# Optimizing a Trainium2 kernel written in Bass

```python
import numpy as np
import jax
import jax.numpy as jnp

def _softmax(x, axis=-1):
    return jax.nn.softmax(x, axis=axis)

def _gelu(x):
    return jax.nn.gelu(x, approximate=True)

def _silu(x):
    return jax.nn.silu(x)

def _sigmoid(x):
    return jax.nn.sigmoid(x)

def _layernorm(x, axis=-1, eps=1e-05):
    m = jnp.mean(x, axis=axis, keepdims=True)
    v = jnp.var(x, axis=axis, keepdims=True)
    return (x - m) / jnp.sqrt(v + eps)

def _scatter_add(tgt, idx, src, axis=0):
    return tgt.at[idx].add(src)

def _segment_sum(src, seg, n):
    return jax.ops.segment_sum(src, seg, n)
kernel_name = 'mk_cond_resid_d1_seqx_r2_f8b336'

def setup_inputs(seed: int=0):
    np.random.seed(seed)
    _w = jnp.asarray

    def _rec_inputs():
        import jax
        import jax.numpy as jnp
        _rk = jax.random.key(seed)
        x = -0.000125 + 0.9999 * jax.random.normal(jax.random.fold_in(_rk, 1), (4, 1024, 1024), jnp.float32)
        _lenS = 1024 - jax.random.randint(jax.random.fold_in(_rk, 7), (4,), 0, max(1, 1024 // 4) + 1, jnp.int32)
        _lenS2 = 1024 - jax.random.randint(jax.random.fold_in(_rk, 8), (4,), 0, max(1, 1024 // 4) + 1, jnp.int32)
        cond_2048 = 7.82532e-05 + 0.0100527 * jax.random.normal(jax.random.fold_in(_rk, 11), (4, 1024), jnp.float32)
        return (x, cond_2048)
    x, cond_2048 = _rec_inputs()

    def _L0_cond_setup():
        import jax, jax.numpy as jnp
        import numpy as np
        NUM_BLOCKS = 8
        NUM_LAYERS = 4
        EPS = 1e-06
        key = jax.random.key(seed)
        ks = jax.random.split(key, 6)
        B, S, H = (4, 2048, 1024)
        inputs = jax.random.normal(ks[0], (B, S, H), dtype=jnp.float32)
        query_vectors = jax.random.normal(ks[1], (NUM_LAYERS, H), dtype=jnp.float32) * 0.01
        lim = float(np.sqrt(6.0 / (H + H)))
        Wk = jax.random.uniform(ks[2], (H, H), minval=-lim, maxval=lim, dtype=jnp.float32)
        Wo = jax.random.uniform(ks[3], (H, H), minval=-lim, maxval=lim, dtype=jnp.float32)
        rms_weight = jnp.ones((H,), dtype=jnp.float32)
        ln_gamma = jnp.ones((H,), dtype=jnp.float32)
        ln_beta = jnp.zeros((H,), dtype=jnp.float32)
        return {'inputs': inputs, 'layer_idx': 1, 'rms_weight': rms_weight, 'query_vectors': query_vectors, 'Wk': Wk, 'Wo': Wo, 'ln_gamma': ln_gamma, 'ln_beta': ln_beta}
    _L0_cond_all = _L0_cond_setup()
    _L0_cond_in = {k: v for k, v in _L0_cond_all.items() if k in ('rms_weight', 'Wk', 'Wo', 'ln_gamma', 'ln_beta')}
    del _L0_cond_all
    return {'x': x, 'cond_2048': cond_2048, 'L0_cond_rms_weight': _L0_cond_in['rms_weight'], 'L0_cond_Wk': _L0_cond_in['Wk'], 'L0_cond_Wo': _L0_cond_in['Wo'], 'L0_cond_ln_gamma': _L0_cond_in['ln_gamma'], 'L0_cond_ln_beta': _L0_cond_in['ln_beta']}

def reference(x, cond_2048, L0_cond_rms_weight, L0_cond_Wk, L0_cond_Wo, L0_cond_ln_gamma, L0_cond_ln_beta):
    import jax
    import jax.numpy as jnp

    def _L0_cond_ref(inputs, layer_idx, rms_weight, query_vectors, Wk, Wo, ln_gamma, ln_beta):
        import jax, jax.numpy as jnp
        import numpy as np
        NUM_BLOCKS = 8
        NUM_LAYERS = 4
        EPS = 1e-06
        B, S, H = inputs.shape
        block_size = max(1, S // NUM_BLOCKS)
        n_blocks = S // block_size
        block_repr = inputs.reshape(B, n_blocks, block_size, H).sum(axis=2)
        keys = jnp.einsum('bnh,kh->bnk', block_repr, Wk)
        rms = jnp.sqrt(jnp.mean(keys * keys, axis=-1, keepdims=True) + EPS)
        keys = keys / rms * rms_weight
        q = query_vectors[layer_idx]
        scores = jnp.einsum('bnh,h->bn', keys, q)
        attn = jax.nn.softmax(scores, axis=-1)
        attended = jnp.einsum('bn,bnh->bh', attn, block_repr)
        attended = jnp.broadcast_to(attended[:, None, :], (B, S, H))
        proj = jnp.einsum('bsh,kh->bsk', attended, Wo)
        x = inputs + proj
        mu = jnp.mean(x, axis=-1, keepdims=True)
        var = jnp.mean((x - mu) ** 2, axis=-1, keepdims=True)
        out = (x - mu) / jnp.sqrt(var + EPS) * ln_gamma + ln_beta
        return out
    x = x + _L0_cond_ref(x, 1, L0_cond_rms_weight, cond_2048, L0_cond_Wk, L0_cond_Wo, L0_cond_ln_gamma, L0_cond_ln_beta)
    return x

_drawn_inputs = setup_inputs


def setup_inputs(seed=0):
    import zlib

    import numpy as np

    out = dict(_drawn_inputs(seed))
    spreads = {'L0_cond_rms_weight': (1.0, 0.6),
     'L0_cond_ln_gamma': (1.0, 0.2),
     'L0_cond_ln_beta': (0.0, 0.1)}
    factors = {}
    for name, (base, spread) in spreads.items():
        noise = np.random.default_rng([zlib.crc32(name.encode()), seed]).standard_normal(out[name].shape)
        drawn = base * np.exp(spread * noise) if base else spread * noise
        out[name] = jnp.asarray(drawn.astype(out[name].dtype))
    for name, factor in factors.items():
        out[name] = (out[name] * factor).astype(out[name].dtype)
    return out
```

```python
import concourse.bass as bass
from concourse import mybir
from contextlib import ExitStack

F32 = mybir.dt.float32
BF16 = mybir.dt.bfloat16
ALU = mybir.AluOpType
ACT = mybir.ActivationFunctionType
AX = mybir.AxisListType

LAYER = 1
NUM_BLOCKS = 8
EPS = 1e-6


def bass_block_attention_residual_norm_kernel(
    nc: bass.Bass,
    x: bass.AP,
    cond: bass.AP,
    rms_weight: bass.AP,
    Wk: bass.AP,
    Wo: bass.AP,
    gamma: bass.AP,
    beta: bass.AP,
    out: bass.AP,
):
    B, S, H = x.shape
    P = 128
    NT = S // P
    HC = H // P
    HALF = H // 2
    QK = H // 4
    G = 4
    NG = NT // G
    KR = 32
    KU = 24
    ROW_M, ROW_ONE, ROW_P = 9, 18, 21
    assert S // NUM_BLOCKS == P and NT == 8 and HC == 8 and HALF == 512 and B == 4

    x_dram = x.rearrange("b (n p) h -> b p n h", p=P)
    out_dram = out.rearrange("b (n p) h -> p (b n) h", p=P)
    BLOCKS = [0, 2, 4, 6, 1, 3, 5, 7]
    wk_dram = Wk.rearrange("(k p) h -> p k h", p=P)
    wo_dram = Wo.rearrange("(k p) h -> p k h", p=P)

    with ExitStack() as ctx:
        def sb(name, shape, dt=F32):
            return ctx.enter_context(nc.sbuf_tensor(name, shape, dt))

        def pb(name, shape, dt=F32):
            return ctx.enter_context(nc.psum_tensor(name, shape, dt))

        def sem(name):
            return ctx.enter_context(nc.semaphore(name))

        X = sb("X", [P, B * NT * H])
        WkT = sb("WkT", [P, HC, H])
        WoT = sb("WoT", [P, HC, H])
        Pb = sb("Pb", [P, 2 * H])
        x2 = sb("x2", [P, 2, H])
        ROWS = sb("ROWS", [2 * KR, 2 * H], BF16)
        RA, RC = ROWS[0:KR, 0:H], ROWS[KR:2 * KR, :]
        rT = sb("rT", [P, HC, 32])
        LT = sb("LT", [2 * KR, 2, G * P], BF16)
        identF = sb("identF", [P, P])
        identB = sb("identB", [P, P], BF16)
        MC = sb("MC", [P, HC, KR], BF16)
        rowjunk = sb("rowjunk", [P, H], BF16)
        vv = sb("vv", [P, QK])
        psel = sb("psel", [2 * KR, P], BF16)
        fold = sb("fold", [P, 32])
        ones = sb("ones", [P, 35])
        qmask = sb("qmask", [P, 4])
        GB = sb("GB", [P, 2, HC])
        gbp = sb("gbp", [P, 3, 2, HC], BF16)
        pp = sb("pp", [P, 2, HC])
        pd = sb("pd", [P, 2, HC])
        ppp = sb("ppp", [P, 3, 2, HC], BF16)
        eps_col = sb("eps_col", [P, 1])
        st = sb("st", [P, 2])
        sumP = sb("sumP", [P, 2])
        negx = sb("negx", [P, B * NT])
        negmu = sb("negmu", [P, B * NT])
        sqs = sb("sqs", [P, B * NT])
        r0 = sb("r0", [P, B * NT])
        var = sb("var", [P, G])
        nt1 = sb("nt1", [P, G])
        nt2 = sb("nt2", [P, G])
        RM = sb("RM", [P, G, 2])
        RMd = sb("RMd", [P, G, 2])
        SM = sb("SM", [P, G, KR], BF16)
        row = sb("row", [1, 64])
        arow = sb("arow", [1, P])
        acol = sb("acol", [P, 4])
        sc = [sb(f"sc{i}", [1, 8]) for i in range(8)]
        one1 = sb("one1", [1, 1])

        psA = pb("psA", [P, H])
        psC = pb("psC", [P, H])
        psB = pb("psB", [P, H])
        ps6 = pb("ps6", [P, HALF])
        ps7 = pb("ps7", [P, H], BF16)
        ps6h = ps6[:, :].bitcast(BF16)
        ps7f = ps7[:, :].bitcast(F32)

        x_landed = [sem(f"x_landed{b}") for b in range(B)]
        wk_landed = [sem(f"wk_landed{m}") for m in range(4)]
        wo_landed = [sem(f"wo_landed{m}") for m in range(4)]
        small_landed = sem("small_landed")
        stored = sem("stored")
        consts_done = sem("consts_done")
        const_step = sem("const_step")
        dconst = sem("dconst")
        gb_psum = sem("gb_psum")
        ma_ready = sem("ma_ready")
        ra_psum = sem("ra_psum")
        w_psum = sem("w_psum")
        w_act = sem("w_act")
        w_dve = sem("w_dve")
        r_summed = sem("r_summed")
        r_copied = sem("r_copied")
        rt_psum = sem("rt_psum")
        rt_copied = sem("rt_copied")
        k_done = sem("k_done")
        v_done = sem("v_done")
        v_copied = sem("v_copied")
        kv_scored = sem("kv_scored")
        kk_summed = sem("kk_summed")
        rows_psum = sem("rows_psum")
        row_step = sem("row_step")
        row_act = sem("row_act")
        acol_psum = sem("acol_psum")
        pt_psum = sem("pt_psum")
        rc_psum = sem("rc_psum")
        rc_ready = sem("rc_ready")
        pb_psum = sem("pb_psum")
        p_ready = sem("p_ready")
        nmu_step = sem("nmu_step")
        rowsum_done = sem("rowsum_done")
        x2_done = sem("x2_done")
        sq_done = sem("sq_done")
        r0_step = sem("r0_step")
        stat_step = sem("stat_step")
        lt_psum = sem("lt_psum")
        lt_ready = sem("lt_ready")
        a_ready = sem("a_ready")
        c_ready = sem("c_ready")
        mult_done = sem("mult_done")
        final_done = sem("final_done")

        N_CONST = 5
        ROW_STEPS = 19
        STAT_STEPS = 9

        block = ctx.enter_context(nc.Block())

        def x_tile(b, j, lo=0, n=H):
            return X[:, bass.ds((b * NT + j) * H + lo, n)]

        @block.sync
        def _(sp):
            def stage(b):
                return X[:, b * NT * H:(b + 1) * NT * H].rearrange("p (n h) -> p n h", h=H)

            def load_x(b):
                sp.dma_start(stage(b), x_dram[b]).then_inc(x_landed[b], 16)

            load_x(0)
            for dram, at, landed in ((wk_dram, 2, wk_landed), (wo_dram, 3, wo_landed)):
                for m in range(4):
                    k0 = BLOCKS[2 * m]
                    sp.dma_start(stage(at)[:, k0:k0 + 3:2, :], dram[:, k0:k0 + 3:2, :]).then_inc(landed[m], 16)
            load_x(1)
            sp.wait_ge(w_psum, HC)
            load_x(2)
            sp.wait_ge(w_psum, 2 * HC)
            load_x(3)
            with sp.Fori(0, B * NT // 2 - 1) as i:
                sp.wait_ge(final_done, 2 * i + 2)
                sp.dma_start(out_dram[:, bass.ds(2 * i, 2), :],
                             X[:, bass.ds(2 * i * H, 2 * H)].rearrange("p (n h) -> p n h", h=H)).then_inc(stored, 16)
            for t in range(B * NT - 2, B * NT):
                sp.wait_ge(final_done, t + 1)
                sp.dma_start(out_dram[:, t, :], X[:, t * H:(t + 1) * H]).then_inc(stored, 16)
            sp.wait_ge(stored, 16 * (B * NT // 2 + 1))

        @block.gpsimd
        def _(pool):
            pool.memset(identF[:, :], 0.0).then_inc(const_step, 1)
            pool.memset(fold[:, :], 0.0).then_inc(const_step, 1)
            pool.memset(qmask[:, :], 1.0).then_inc(const_step, 1)
            pool.memset(psel[:, :], 1.0).then_inc(const_step, 1)
            pool.memset(ones[:, :], 0.0).then_inc(const_step, 1)
            pool.memset(eps_col[:, :], EPS).then_inc(consts_done, 1)
            pool.memset(one1[:, :], 1.0).then_inc(consts_done, 1)
            pool.memset(arow[:, :], 0.0).then_inc(consts_done, 1)
            pool.wait_ge(const_step, 5)
            pool.memset(ones[:, 3:4], 1.0).then_inc(consts_done, 1)
            pool.affine_select(out=identF[:, :], in_=identF[:, :], compare_op=ALU.not_equal, fill=1.0,
                               base=0, pattern=[[-1, P]], channel_multiplier=1).then_inc(const_step, 1)
            pool.affine_select(out=psel[:, :], in_=psel[:, :], compare_op=ALU.is_ge, fill=0.0,
                               base=-KR - ROW_P, pattern=[[0, P]], channel_multiplier=1).then_inc(const_step, 1)
            pool.affine_select(out=qmask[:, :], in_=qmask[:, :], compare_op=ALU.is_ge, fill=0.0,
                               base=0, pattern=[[-32, 4]], channel_multiplier=1).then_inc(const_step, 1)
            pool.wait_ge(const_step, 8)
            pool.affine_select(out=qmask[:, :], in_=qmask[:, :], compare_op=ALU.is_ge, fill=0.0,
                               base=31, pattern=[[32, 4]], channel_multiplier=-1).then_inc(const_step, 1)
            for q in range(4):
                if q:
                    pool.wait_ge(const_step, 9 + q)
                pool.affine_select(out=fold[:, :], in_=fold[:, :], compare_op=ALU.not_equal, fill=1.0,
                                   base=-32 * q, pattern=[[-1, 32]], channel_multiplier=1).then_inc(const_step, 1)
            pool.wait_ge(const_step, 13)
            pool.memset(rowjunk[0:1, 0:1], 0.0).then_inc(consts_done, 1)

            def add_p(b):
                for j in range(NT):
                    if not (isinstance(b, int) and b == 0 and j < 2):
                        pool.wait_ge(sq_done, b * NT + j - 1)
                    pool.tensor_tensor(x2[:, j % 2, :], x_tile(b, j), Pb[:, bass.ds((b % 2) * H, H)],
                                       ALU.add).then_inc(x2_done, 1)

            pool.wait_ge(p_ready, 1)
            add_p(0)
            with pool.Fori(1, B) as b:
                pool.wait_ge(p_ready, b + 1)
                add_p(b)

        @block.scalar
        def _(act):
            act.preload_act_table_set("natural_log_exp_and_others")
            GBrow = x2[0:2 * HC, 0, 0:P]
            act.dma_start(x2[0:HC, 0, 0:P], gamma.rearrange("(c p) -> c p", p=P)).then_inc(small_landed, 16)
            act.dma_start(x2[HC:2 * HC, 0, 0:P], beta.rearrange("(c p) -> c p", p=P)).then_inc(small_landed, 16)
            for q in range(4):
                for src, at in ((cond[LAYER:LAYER + 1, q * QK:(q + 1) * QK], 0),
                                (rms_weight.rearrange("(o h) -> o h", o=1)[:, q * QK:(q + 1) * QK], QK)):
                    act.dma_start(x2[32 * q:32 * q + 32, 1, at:at + QK],
                                  src.broadcast_to([32, QK])).then_inc(small_landed, 16)

            def rowsum(b, j, landed=None):
                if landed is not None:
                    act.wait_ge(landed, 16)
                if not (isinstance(b, int) and b == 0 and j == 0):
                    act.wait_ge(rowsum_done, b * NT + j)
                act.activation(rowjunk[:, :], x_tile(b, j), ACT.Copy, scale=-1.0 / H,
                               accum_out=negx[:, bass.ds(b * NT + j, 1)]).then_inc(rowsum_done, 1)

            def r_copy(b):
                act.wait_ge(r_summed, b + 1)
                if not (isinstance(b, int) and b < 2):
                    act.wait_ge(x2_done, (b - 1) * NT)
                act.activation(Pb[:, bass.ds((b % 2) * H, HALF)], psB[:, 0:HALF], ACT.Copy).then_inc(r_copied, 1)

            def v_copy(b):
                act.wait_ge(v_done, b + 1)
                act.activation(Pb[:, bass.ds((b % 2) * H + HALF, QK)], psB[:, HALF:HALF + QK],
                               ACT.Copy).then_inc(v_copied, 1)

            def kk_sum(b):
                act.wait_ge(kv_scored, b + 1)
                act.activation(Pb[:, bass.ds((b % 2) * H, QK)], psB[:, 0:QK], ACT.Square,
                               accum_out=st[:, 1:2]).then_inc(kk_summed, 1)

            def key_rms(b):
                act.wait_ge(row_step, ROW_STEPS * b + 2)
                act.activation(sc[1][:, :], sc[0][:, :], ACT.Ln).then_inc(row_act, 1)
                act.wait_ge(row_act, 4 * b + 1)
                act.activation(sc[2][:, :], sc[1][:, :], ACT.Exp, scale=-0.5).then_inc(row_act, 1)

            def softmax_exp(b):
                act.wait_ge(row_step, ROW_STEPS * b + 8)
                act.activation(sc[6][:, :], sc[5][:, :], ACT.Exp, accum_out=sc[7][:, 0:1]).then_inc(row_act, 2)

            def p_copy(b):
                act.wait_ge(pb_psum, b + 1)
                act.activation(Pb[:, bass.ds((b % 2) * H, H)], psB[:, :], ACT.Copy,
                               accum_out=sumP[:, 0:1]).then_inc(p_ready, 1)

            def neg_mu(b):
                act.wait_ge(p_ready, b + 1)
                act.activation(sumP[:, 1:2], sumP[:, 0:1], ACT.Copy, scale=-1.0 / H).then_inc(nmu_step, 1)
                act.wait_ge(nmu_step, 2 * b + 1)
                act.wait_ge(rowsum_done, (b + 1) * NT)
                act.activation(negmu[:, bass.ds(b * NT, NT)], negx[:, bass.ds(b * NT, NT)], ACT.Identity,
                               bias=sumP[:, 1:2]).then_inc(nmu_step, 1)
                act.wait_ge(nmu_step, 2 * b + 2)

            def square(b, j):
                act.wait_ge(x2_done, b * NT + j + 1)
                act.activation(x2[:, j % 2, :], x2[:, j % 2, :], ACT.Square,
                               bias=negmu[:, bass.ds(b * NT + j, 1)],
                               accum_out=sqs[:, bass.ds(b * NT + j, 1)]).then_inc(sq_done, 1)

            def first_rstd(b, g):
                at = bass.ds(b * NT + g * G, G)
                act.wait_ge(sq_done, b * NT + (g + 1) * G)
                act.activation(r0[:, at], sqs[:, at], ACT.Ln, scale=1.0 / H, bias=eps_col[:, :]).then_inc(r0_step, 1)
                act.wait_ge(r0_step, 2 * (NG * b + g) + 1)
                act.activation(r0[:, at], r0[:, at], ACT.Exp, scale=-0.5).then_inc(r0_step, 1)

            act.wait_ge(consts_done, N_CONST)
            rowsum(0, 0, x_landed[0])
            r_copy(0)
            for j in range(1, NT):
                rowsum(0, j)
            for m in range(0, 2 * HC, 2):
                act.wait_ge(w_psum, m + 1)
                WT = WkT if m < HC else WoT
                k = BLOCKS[m % HC]
                act.activation(WT[:, :, k * P:(k + 1) * P], psA[:, :].rearrange("p (c k) -> p c k", c=HC),
                               ACT.Copy).then_inc(w_act, 1)
                if m == HC:
                    kk_sum(0)
            v_copy(0)
            key_rms(0)
            softmax_exp(0)
            p_copy(0)

            def batch(b, more, landed=None):
                neg_mu(b)
                for j in range(NT):
                    square(b, j)
                    if j == G - 1:
                        first_rstd(b, 0)
                    if more:
                        if j == 1:
                            r_copy(b + 1)
                        if j == 3:
                            kk_sum(b + 1)
                        if j == 4:
                            v_copy(b + 1)
                            key_rms(b + 1)
                        if j == 5:
                            softmax_exp(b + 1)
                        if j == 6:
                            p_copy(b + 1)
                        rowsum(b + 1, j, landed)
                first_rstd(b, 1)

            batch(0, True, x_landed[1])
            batch(1, True, x_landed[2])
            batch(2, True, x_landed[3])
            batch(3, False)

        @block.vector
        def _(dve):
            steps = [0]

            def const(ins):
                ins.then_inc(dconst, 1)
                steps[0] += 1
                dve.wait_ge(dconst, steps[0])

            dve.wait_ge(consts_done, N_CONST)
            const(dve.tensor_copy(identB[:, :], identF[:, :]))
            const(dve.memset(MC[:, :, :], 0.0))
            const(dve.memset(SM[:, :, :], 0.0))
            dve.memset(SM[:, :, ROW_ONE:ROW_ONE + 3], 1.0).then_inc(dconst, 1)
            steps[0] += 1
            dve.wait_ge(small_landed, 160)
            const(dve.tensor_tensor(vv[:, :], x2[:, 1, 0:QK], x2[:, 1, QK:2 * QK], ALU.mult))
            dve.wait_ge(gb_psum, 1)
            const(dve.tensor_copy(GB[:, :, :], ps6[:, 0:2 * HC].rearrange("p (v c) -> p v c", v=2)))
            const(dve.tensor_copy(gbp[:, 0, :, :], GB[:, :, :]))
            const(dve.tensor_tensor(pp[:, :, :], GB[:, :, :], gbp[:, 0, :, :], ALU.subtract))
            const(dve.tensor_copy(gbp[:, 1, :, :], pp[:, :, :]))
            const(dve.tensor_tensor(gbp[:, 2, :, :], pp[:, :, :], gbp[:, 1, :, :], ALU.subtract))

            def part_rows(v, at, reps):
                return (MC[:, :, at:at + 3 * reps].rearrange("p c (i j) -> p c i j", j=3),
                        gbp[:, :, v, :].rearrange("p j c -> p c j").unsqueeze(2).broadcast_to([P, HC, reps, 3]))

            o, i = part_rows(0, 0, 3)
            const(dve.tensor_copy(o, i))
            const(dve.memset(MC[:, :, ROW_ONE:ROW_ONE + 1], 1.0))
            dve.sem_inc(ma_ready, 1)
            dve.wait_ge(ra_psum, 1)
            const(dve.tensor_copy(RA, ps7[0:KR, :]))
            o, i = part_rows(0, ROW_M, 3)
            const(dve.tensor_copy(o, i))
            o, i = part_rows(1, ROW_ONE, 1)
            const(dve.tensor_copy(o, i))

            def rt_copy(b):
                dve.wait_ge(rt_psum, b + 1)
                src = psB[:, HALF:H].rearrange("p (c f u i) -> p c f u i", f=2, u=2, i=32)
                for f in range(2):
                    dst = rT[:, 4 * f:4 * f + 4, :].rearrange("p c (u i) -> p c u i", u=2)
                    dve.tensor_copy(dst, src[:, :, f, :, 0:16]).then_inc(rt_copied, 1)

            def score(b):
                dve.wait_ge(k_done, b + 1)
                dve.scalar_tensor_tensor(out=Pb[:, bass.ds((b % 2) * H + HALF + QK, QK)], in0=psB[:, 0:QK],
                                         scalar=1.0, in1=vv[:, :], op0=ALU.mult, op1=ALU.mult,
                                         accum_out=st[:, 0:1]).then_inc(kv_scored, 1)

            def row_ops(b):
                return lambda ins: ins.then_inc(row_step, 1), lambda n: dve.wait_ge(row_step, ROW_STEPS * b + n)

            def view8(ap):
                return ap.rearrange("o (u i) -> o u i", u=2)

            def row_a(b):
                done, after = row_ops(b)
                dve.wait_ge(rows_psum, b + 1)
                done(dve.tensor_copy(row[:, :], ps6[0:1, 0:64]))
                after(1)
                ss = row[:, 32:64].rearrange("o (u i) -> o u i", u=2)[:, :, 0:4]
                done(dve.tensor_scalar(view8(sc[0][:, :]), ss, 1.0 / H, EPS, ALU.mult, ALU.add))

            def row_b(b):
                done, after = row_ops(b)
                s = row[:, 0:32].rearrange("o (u i) -> o u i", u=2)[:, :, 0:4]
                dve.wait_ge(row_act, 4 * b + 2)
                done(dve.scalar_tensor_tensor(out=sc[3][:, :], in0=sc[0][:, :], scalar=-0.5, in1=sc[2][:, :],
                                              op0=ALU.mult, op1=ALU.mult))
                after(3)
                done(dve.tensor_tensor(sc[4][:, :], sc[3][:, :], sc[2][:, :], ALU.mult))
                after(4)
                done(dve.scalar_tensor_tensor(out=sc[1][:, :], in0=sc[4][:, :], scalar=1.5, in1=sc[2][:, :],
                                              op0=ALU.add, op1=ALU.mult))
                after(5)
                done(dve.tensor_tensor(view8(sc[3][:, :]), s, view8(sc[1][:, :]), ALU.mult))
                after(6)
                done(dve.reduce_max(sc[4][:, 0:1], sc[3][:, :], AX.X))
                after(7)
                done(dve.tensor_scalar(sc[5][:, :], sc[3][:, :], sc[4][:, 0:1], None, ALU.subtract))

            def row_c(b):
                done, after = row_ops(b)
                dve.wait_ge(row_act, 4 * b + 4)
                done(dve.reciprocal(sc[7][:, 1:2], sc[7][:, 0:1]))
                after(9)
                dst = arow[:, :].rearrange("o (q u i) -> o q u i", q=4, u=2)[:, :, :, 0:4]
                src = view8(sc[6][:, :]).unsqueeze(1).broadcast_to([1, 4, 2, 4])
                done(dve.tensor_scalar(dst, src, sc[7][:, 1:2], None, ALU.mult))

            def col_a(b):
                done, after = row_ops(b)
                dve.wait_ge(acol_psum, b + 1)
                done(dve.tensor_tensor(acol[:, :], qmask[:, :], ps7f[:, 0:1].broadcast_to([P, 4]), ALU.mult))

            def col_b(b):
                done, after = row_ops(b)
                dve.wait_ge(pt_psum, b + 1)
                pt = ps6[:, 0:HC].rearrange("p (s q) -> p q s", s=2)
                kc = lambda ap: ap.rearrange("p (q s) -> p q s", s=2)
                done(dve.tensor_copy(kc(pp[:, 0, :]), pt))
                done(dve.tensor_tensor(kc(pp[:, 1, :]), pt, kc(GB[:, 0, :]), ALU.mult))
                after(13)
                done(dve.tensor_copy(ppp[:, 0, :, :], pp[:, :, :]))
                after(14)
                done(dve.tensor_tensor(pd[:, :, :], pp[:, :, :], ppp[:, 0, :, :], ALU.subtract))
                after(15)
                done(dve.tensor_copy(ppp[:, 1, :, :], pd[:, :, :]))
                after(16)
                done(dve.tensor_tensor(ppp[:, 2, :, :], pd[:, :, :], ppp[:, 1, :, :], ALU.subtract))
                after(17)
                part = lambda v: ppp[:, :, v, :].rearrange("p j c -> p c j")
                done(dve.tensor_copy(MC[:, :, ROW_P:ROW_P + 3], part(0)))
                done(dve.tensor_copy(MC[:, :, 0:9].rearrange("p c (i j) -> p c i j", j=3),
                                     part(1).unsqueeze(2).broadcast_to([P, HC, 3, 3])))

            def rc_copy(b):
                dve.wait_ge(rc_psum, b + 1)
                dve.tensor_copy(ROWS[KR:2 * KR, bass.ds((b % 2) * H, H)], ps7[KR:2 * KR, :]).then_inc(rc_ready, 1)

            def stats(b, g):
                gi = NG * b + g
                at = bass.ds(b * NT + g * G, G)
                done = lambda ins: ins.then_inc(stat_step, 1)
                after = lambda n: dve.wait_ge(stat_step, STAT_STEPS * gi + n)
                dve.wait_ge(r0_step, 2 * (gi + 1))
                done(dve.tensor_scalar(var[:, :], sqs[:, at], 1.0 / H, EPS, ALU.mult, ALU.add))
                after(1)
                done(dve.scalar_tensor_tensor(out=nt1[:, :], in0=var[:, :], scalar=-0.5, in1=r0[:, at],
                                              op0=ALU.mult, op1=ALU.mult))
                after(2)
                done(dve.tensor_tensor(nt2[:, :], nt1[:, :], r0[:, at], ALU.mult))
                after(3)
                done(dve.scalar_tensor_tensor(out=RM[:, :, 0], in0=nt2[:, :], scalar=1.5, in1=r0[:, at],
                                              op0=ALU.add, op1=ALU.mult))
                after(4)
                done(dve.tensor_tensor(RM[:, :, 1], RM[:, :, 0], negmu[:, at], ALU.mult))
                after(5)
                part = lambda i: SM[:, :, 0:18].rearrange("p t (v i j) -> p t v i j", i=3, j=3)[:, :, :, i, :]
                rep = lambda ap: ap.unsqueeze(3).broadcast_to([P, G, 2, 3])
                done(dve.tensor_copy(part(0), rep(RM[:, :, :])))
                after(6)
                done(dve.tensor_tensor(RMd[:, :, :], RM[:, :, :], part(0)[:, :, :, 0], ALU.subtract))
                after(7)
                done(dve.tensor_copy(part(1), rep(RMd[:, :, :])))
                after(8)
                done(dve.tensor_tensor(part(2), rep(RMd[:, :, :]), part(1), ALU.subtract))
                dve.wait_ge(lt_psum, gi + 1)
                dve.tensor_copy(LT[:, g, :], ps6h[0:2 * KR, 0:G * P]).then_inc(lt_ready, 1)

            def mult(b, j):
                dve.wait_ge(a_ready, b * NT + j + 1)
                dve.tensor_tensor(x_tile(b, j), x_tile(b, j), psA[:, :], ALU.mult).then_inc(mult_done, 1)

            def add(b, j):
                dve.wait_ge(c_ready, b * NT + j + 1)
                dve.wait_ge(mult_done, b * NT + j + 1)
                dve.tensor_tensor(x_tile(b, j), x_tile(b, j), psC[:, :], ALU.add).then_inc(final_done, 1)

            rt_copy(0)
            for m in range(1, 2 * HC, 2):
                dve.wait_ge(w_psum, m + 1)
                WT = WkT if m < HC else WoT
                k = BLOCKS[m % HC]
                dve.tensor_copy(WT[:, :, k * P:(k + 1) * P],
                                psC[:, :].rearrange("p (c k) -> p c k", c=HC)).then_inc(w_dve, 1)
                if m == HC + 1:
                    score(0)
            row_a(0)
            row_b(0)
            row_c(0)
            col_a(0)
            col_b(0)
            rc_copy(0)
            rt_copy(1)
            score(1)

            def batch(b, chain_b, chain_a):
                stats(b, 0)
                mult(b, 0)
                if chain_b:
                    row_a(b + 1)
                add(b, 0)
                if chain_b:
                    row_b(b + 1)
                mult(b, 1)
                if chain_b:
                    row_c(b + 1)
                add(b, 1)
                if chain_b:
                    col_a(b + 1)
                mult(b, 2)
                if chain_b:
                    col_b(b + 1)
                add(b, 2)
                mult(b, 3)
                if chain_b:
                    rc_copy(b + 1)
                add(b, 3)
                stats(b, 1)
                mult(b, 4)
                add(b, 4)
                mult(b, 5)
                if chain_a:
                    rt_copy(b + 2)
                add(b, 5)
                mult(b, 6)
                add(b, 6)
                if chain_a:
                    score(b + 2)
                mult(b, 7)
                add(b, 7)

            with dve.Fori(0, B - 2) as b:
                batch(b, True, True)
            batch(B - 2, True, False)
            batch(B - 1, False, False)

        @block.tensor
        def _(pe):
            mm = nc.tensor.matmul

            def sums(b):
                if b:
                    pe.wait_ge(p_ready, b)
                pe.wait_ge(x_landed[b], 16)
                for i in range(NT // 2):
                    for f in range(2):
                        for u in range(2):
                            q = 2 * f + u
                            at = (b * NT + 2 * i + u) * H + f * HALF
                            last = mm(psB[32 * q:32 * q + 32, 0:HALF], ones[:, 3 - i:35 - i],
                                      X[:, at:at + HALF], start=(i == 0), stop=(i == NT // 2 - 1))
                last.then_inc(r_summed, 1)

            def sums_t(b):
                pe.wait_ge(r_copied, b + 1)
                at = (b % 2) * H
                for c in range(4):
                    last = nc.tensor.transpose(psB[:, HALF + c * P:HALF + (c + 1) * P],
                                               Pb[:, at + c * P:at + (c + 1) * P], identF[:, :])
                last.then_inc(rt_psum, 1)

            def times_w(at, WT, sub, n, done=None):
                for c in range(HC):
                    for q in range(4):
                        k = q * QK + sub * P
                        last = mm(psB[32 * q:32 * q + 32, at + sub * P:at + sub * P + n], rT[:, c, :],
                                  WT[:, c, k:k + n], start=(c == 0), stop=(c == HC - 1))
                if done is not None:
                    last.then_inc(done, 1)

            def keys(b):
                pe.wait_ge(rt_copied, 2 * (b + 1))
                times_w(0, WkT, 0, QK, k_done)

            def values(b):
                times_w(HALF, WoT, 0, QK, v_done)

            def rows(b):
                pe.wait_ge(kv_scored, b + 1)
                pe.wait_ge(kk_summed, b + 1)
                mm(ps6[0:1, 0:32], st[:, 0:1], fold[:, :], start=True, stop=True)
                mm(ps6[0:1, 32:64], st[:, 1:2], fold[:, :], start=True, stop=True).then_inc(rows_psum, 1)

            def attn_col(b):
                pe.wait_ge(row_step, ROW_STEPS * b + 10)
                if b:
                    pe.wait_ge(rc_ready, b)
                mm(ps7f[:, 0:1], arow[:, :], one1[:, :], start=True, stop=True).then_inc(acol_psum, 1)

            def p_col(b):
                pe.wait_ge(row_step, ROW_STEPS * b + 11)
                pe.wait_ge(v_copied, b + 1)
                for s in range(2):
                    at = (b % 2) * H + HALF + s * P
                    last = mm(ps6[:, 4 * s:4 * s + 4], Pb[:, at:at + P], acol[:, :], start=True, stop=True)
                last.then_inc(pt_psum, 1)

            def part_rows(lo, done):
                for c in range(HC):
                    last = nc.tensor.transpose(ps7[lo:lo + KR, c * P:(c + 1) * P], MC[:, c, :], identB[:, :])
                last.then_inc(done, 1)

            def c_rows(b):
                pe.wait_ge(row_step, ROW_STEPS * (b + 1))
                part_rows(KR, rc_psum)

            def p_rows(b):
                pe.wait_ge(rc_ready, b + 1)
                for f in range(2):
                    at = (b % 2) * H + f * HALF
                    last = mm(psB[:, f * HALF:(f + 1) * HALF], psel[KR:KR + KU, :], ROWS[KR:KR + KU, at:at + HALF],
                              start=True, stop=True)
                last.then_inc(pb_psum, 1)

            def stat_rows(b, g):
                gi = NG * b + g
                pe.wait_ge(stat_step, STAT_STEPS * (gi + 1))
                for t in range(G):
                    for lo in (0, KR):
                        last = nc.tensor.transpose(ps6h[lo:lo + KR, t * P:(t + 1) * P], SM[:, t, :], identB[:, :])
                last.then_inc(lt_psum, 1)

            def outer(b, j, ps, lo, at, ready, freed):
                t = b * NT + j
                pe.wait_ge(lt_ready, NG * b + j // G + 1)
                if t:
                    pe.wait_ge(freed, t)
                for f in range(2):
                    last = mm(ps[:, f * HALF:(f + 1) * HALF], LT[lo:lo + KU, j // G, (j % G) * P:(j % G + 1) * P],
                              ROWS[lo:lo + KU, at + f * HALF:at + (f + 1) * HALF], start=True, stop=True)
                last.then_inc(ready, 1)

            def a_tile(b, j):
                outer(b, j, psA, 0, 0, a_ready, mult_done)

            def c_tile(b, j):
                outer(b, j, psC, KR, (b % 2) * H, c_ready, final_done)

            pe.wait_ge(consts_done, N_CONST)
            pe.wait_ge(small_landed, 160)
            nc.tensor.transpose(ps6[:, 0:2 * HC], x2[0:2 * HC, 0, 0:P], identF[0:2 * HC, 0:2 * HC]).then_inc(gb_psum, 1)
            pe.wait_ge(ma_ready, 1)
            part_rows(0, ra_psum)
            sums(0)
            sums_t(0)

            def w_block(m):
                stage, landed = (2, wk_landed) if m < HC else (3, wo_landed)
                k = BLOCKS[m % HC]
                pe.wait_ge(landed[m % HC // 2], 16)
                ps, freed = (psA, w_act) if m % 2 == 0 else (psC, w_dve)
                if m >= 2:
                    pe.wait_ge(freed, m // 2)
                for c in range(HC):
                    at = (stage * NT + k) * H + c * P
                    last = nc.tensor.transpose(ps[:, c * P:(c + 1) * P], X[:, at:at + P], identF[:, :])
                last.then_inc(w_psum, 1)

            for m in range(HC):
                w_block(m)
            pe.wait_ge(w_act, HC // 2)
            pe.wait_ge(w_dve, HC // 2)
            keys(0)
            for m in range(HC, HC + 5):
                w_block(m)
            pe.wait_ge(w_act, HC // 2 + 2)
            pe.wait_ge(w_dve, HC // 2 + 2)
            times_w(HALF, WoT, 0, P)
            for m in range(HC + 5, 2 * HC):
                w_block(m)
            pe.wait_ge(w_act, HC)
            pe.wait_ge(w_dve, HC)
            times_w(HALF, WoT, 1, P, v_done)
            rows(0)
            attn_col(0)
            p_col(0)
            c_rows(0)
            p_rows(0)
            sums(1)
            sums_t(1)
            keys(1)

            for b in range(B):
                chain_b, chain_a = b + 1 < B, b + 2 < B
                stat_rows(b, 0)
                a_tile(b, 0)
                c_tile(b, 0)
                if chain_b:
                    rows(b + 1)
                a_tile(b, 1)
                if chain_b:
                    values(b + 1)
                c_tile(b, 1)
                if chain_b:
                    attn_col(b + 1)
                a_tile(b, 2)
                if chain_b:
                    p_col(b + 1)
                c_tile(b, 2)
                a_tile(b, 3)
                if chain_b:
                    c_rows(b + 1)
                c_tile(b, 3)
                if chain_b:
                    p_rows(b + 1)
                stat_rows(b, 1)
                a_tile(b, 4)
                c_tile(b, 4)
                if chain_a:
                    sums(b + 2)
                a_tile(b, 5)
                c_tile(b, 5)
                if chain_a:
                    sums_t(b + 2)
                a_tile(b, 6)
                if chain_a:
                    keys(b + 2)
                c_tile(b, 6)
                a_tile(b, 7)
                c_tile(b, 7)


_INS = ['x', 'cond_2048', 'L0_cond_rms_weight', 'L0_cond_Wk', 'L0_cond_Wo', 'L0_cond_ln_gamma', 'L0_cond_ln_beta']


def kernel(**inputs):
    import numpy as _np
    import concourse.bacc as _bacc
    from concourse.bass_utils import run_bass_kernel_spmd as _run

    nc = _bacc.Bacc("TRN2", target_bir_lowering=False, num_devices=1, dynamic_dma_scratch_size=1024)
    arrays, args = {}, []
    for name in _INS:
        a = _np.ascontiguousarray(inputs[name])
        arrays[f"in_{name}_dram"] = a
        args.append(nc.dram_tensor(f"in_{name}_dram", a.shape, mybir.dt.from_np(a.dtype), kind="ExternalInput").ap())
    x = inputs['x']
    args.append(nc.dram_tensor("out_0_dram", x.shape, F32, kind="ExternalOutput").ap())
    bass_block_attention_residual_norm_kernel(nc, *args)
    r = _run(nc, [arrays], core_ids=[0])
    return r.results[0]["out_0_dram"]
```

```python
import concourse.bass as bass
from concourse import mybir
from contextlib import ExitStack

F32 = mybir.dt.float32
BF16 = mybir.dt.bfloat16
ALU = mybir.AluOpType
ACT = mybir.ActivationFunctionType
AX = mybir.AxisListType

LAYER = 1
NUM_BLOCKS = 8
EPS = 1e-6


def bass_block_attention_residual_norm_kernel(
    nc: bass.Bass,
    x: bass.AP,
    cond: bass.AP,
    rms_weight: bass.AP,
    Wk: bass.AP,
    Wo: bass.AP,
    gamma: bass.AP,
    beta: bass.AP,
    out: bass.AP,
):
    B, S, H = x.shape
    P = 128
    NT = S // P
    HC = H // P
    HALF = H // 2
    QK = H // 4
    G = 4
    NG = NT // G
    KR = 32
    KU = 24
    ROW_M, ROW_ONE, ROW_P = 9, 18, 21
    assert S // NUM_BLOCKS == P and NT == 8 and HC == 8 and HALF == 512 and B == 4

    x_dram = x.rearrange("b (n p) h -> b p n h", p=P)
    out_dram = out.rearrange("b (n p) h -> p (b n) h", p=P)
    BLOCKS = [0, 2, 4, 6, 1, 3, 5, 7]
    wk_dram = Wk.rearrange("(k p) h -> p k h", p=P)
    wo_dram = Wo.rearrange("(k p) h -> p k h", p=P)

    with ExitStack() as ctx:
        def sb(name, shape, dt=F32):
            return ctx.enter_context(nc.sbuf_tensor(name, shape, dt))

        def pb(name, shape, dt=F32):
            return ctx.enter_context(nc.psum_tensor(name, shape, dt))

        def sem(name):
            return ctx.enter_context(nc.semaphore(name))

        X = sb("X", [P, B * NT * H])
        WkT = sb("WkT", [P, HC, H])
        WoT = sb("WoT", [P, HC, H])
        Pb = sb("Pb", [P, 2 * H])
        x2 = sb("x2", [P, 2, H])
        K3 = 3 * KR
        ROWS = sb("ROWS", [P, 2 * H], BF16)
        RA = ROWS[KR:2 * KR, 0:H]
        C_AT = (0, 2 * KR)
        rT = sb("rT", [P, HC, 32])
        RB = sb("RB", [P, HALF])
        LT = sb("LT", [K3, G * P], BF16)
        identF = sb("identF", [P, P])
        identB = sb("identB", [P, P], BF16)
        MC = sb("MC", [P, HC, KR], BF16)
        rowjunk = sb("rowjunk", [P, H], BF16)
        vv = sb("vv", [P, QK])
        fold = sb("fold", [P, 32])
        ones = sb("ones", [P, 35])
        qmask = sb("qmask", [P, 4])
        quad = WoT[0:4, 0, 0:P]
        attn = sb("attn", [P, P])
        GB = sb("GB", [P, 2, HC])
        gbp = sb("gbp", [P, 3, 2, HC], BF16)
        pp = sb("pp", [P, 2, HC])
        pd = sb("pd", [P, 2, HC])
        ppp = sb("ppp", [P, 3, 2, HC], BF16)
        eps_col = sb("eps_col", [P, 1])
        fence = sb("fence", [1, 1])
        st = sb("st", [P, 2])
        sumP = sb("sumP", [P, 2])
        negx = sb("negx", [P, B * NT])
        negmu = sb("negmu", [P, B * NT])
        sqs = sb("sqs", [P, B * NT])
        r0 = sb("r0", [P, B * NT])
        var = sb("var", [P, G])
        nt1 = sb("nt1", [P, G])
        nt2 = sb("nt2", [P, G])
        RM = sb("RM", [P, G, 2])
        RMd = sb("RMd", [P, G, 2])
        SM = sb("SM", [P, G, KR], BF16)
        spare = ROWS[K3:K3 + 1, 0:H].bitcast(F32)
        arow = spare[:, 0:P]
        orow = spare[:, P:2 * P]
        row = spare[:, 2 * P:2 * P + 64]
        sc = [spare[:, 3 * P + 8 * i:3 * P + 8 * (i + 1)] for i in range(8)]
        acol = sb("acol", [P, 4])

        psA = pb("psA", [P, H])
        psC = pb("psC", [P, H])
        psB = pb("psB", [P, H])
        ps6 = pb("ps6", [P, HALF])
        ps7 = pb("ps7", [P, H], BF16)
        ps6h = ps6[:, :].bitcast(BF16)
        ps7f = ps7[:, :].bitcast(F32)
        psum_attn, psum_rows, psum_pt = ps7f[:, 0:P], ps7f[K3:K3 + 1, P:P + 64], ps7f[:, P + 64:P + 64 + HC]

        x_landed = [[sem(f"x_landed{b}_{f}") for f in range(2)] for b in range(B)]
        wk_landed = [sem(f"wk_landed{m}") for m in range(4)]
        wo_landed = [sem(f"wo_landed{m}") for m in range(4)]
        small_landed = sem("small_landed")
        stored = sem("stored")
        consts_done = sem("consts_done")
        const_step = sem("const_step")
        dconst = sem("dconst")
        gb_psum = sem("gb_psum")
        v_row = sem("v_row")
        ma_ready = sem("ma_ready")
        ra_psum = sem("ra_psum")
        w_psum = sem("w_psum")
        w_act = sem("w_act")
        w_dve = sem("w_dve")
        r_summed = sem("r_summed")
        r_copied = sem("r_copied")
        rt_psum = sem("rt_psum")
        rt_copied = sem("rt_copied")
        k_done = sem("k_done")
        v_done = sem("v_done")
        v_copied = sem("v_copied")
        kv_scored = sem("kv_scored")
        kk_summed = sem("kk_summed")
        rows_psum = sem("rows_psum")
        row_step = sem("row_step")
        row_act = sem("row_act")
        acol_psum = sem("acol_psum")
        pt_psum = sem("pt_psum")
        rc_psum = sem("rc_psum")
        rc_ready = sem("rc_ready")
        ones_ready = sem("ones_ready")
        rows_zeroed = sem("rows_zeroed")
        pb_psum = sem("pb_psum")
        p_halves = sem("p_halves")
        p_ready = sem("p_ready")
        nmu_step = sem("nmu_step")
        rowsum_done = sem("rowsum_done")
        x2_done = sem("x2_done")
        sq_done = sem("sq_done")
        r0_step = sem("r0_step")
        stat_step = sem("stat_step")
        lt_psum = sem("lt_psum")
        lt_ready = sem("lt_ready")
        a_ready = sem("a_ready")
        c_ready = sem("c_ready")
        mult_done = sem("mult_done")
        final_done = sem("final_done")

        N_CONST = 2
        ROW_STEPS = 20
        STAT_STEPS = 9

        BASE = {c: 7 * (c - 2) for c in range(1, B)}

        block = ctx.enter_context(nc.Block())

        def x_tile(b, j, lo=0, n=H):
            return X[:, bass.ds((b * NT + j) * H + lo, n)]

        @block.sync
        def _(sp):
            def stage(b):
                return X[:, b * NT * H:(b + 1) * NT * H].rearrange("p (n h) -> p n h", h=H)

            def load_x(b, f):
                n = slice(f * NT // 2, (f + 1) * NT // 2)
                sp.dma_start(stage(b)[:, n, :], x_dram[b][:, n, :]).then_inc(x_landed[b][f], 16)

            load_x(0, 0)
            for at, src in ((0, gamma), (HC, beta)):
                sp.dma_start(x2[at:at + HC, 0, 0:P], src.rearrange("(c p) -> c p", p=P)).then_inc(small_landed, 16)
            for at, src in ((0, cond[LAYER, :]), (QK, rms_weight)):
                sp.dma_start(x2[0:4, 1, at:at + QK], src.rearrange("(q k) -> q k", q=4)).then_inc(small_landed, 16)
            load_x(0, 1)
            for dram, at, landed in ((wk_dram, 2, wk_landed), (wo_dram, 3, wo_landed)):
                for m in range(4):
                    k0 = BLOCKS[2 * m]
                    sp.dma_start(stage(at)[:, k0:k0 + 3:2, :], dram[:, k0:k0 + 3:2, :]).then_inc(landed[m], 16)
            load_x(1, 0)
            load_x(1, 1)
            sp.wait_ge(w_psum, 2 * HC)
            load_x(2, 0)
            load_x(2, 1)
            sp.wait_ge(w_psum, 4 * HC)
            load_x(3, 0)
            load_x(3, 1)
            with sp.Fori(0, B * NT // 2 - 1) as i:
                sp.wait_ge(final_done, 2 * i + 2)
                sp.dma_start(out_dram[:, bass.ds(2 * i, 2), :],
                             X[:, bass.ds(2 * i * H, 2 * H)].rearrange("p (n h) -> p n h", h=H)).then_inc(stored, 16)
            for t in range(B * NT - 2, B * NT):
                sp.wait_ge(final_done, t + 1)
                sp.dma_start(out_dram[:, t, :], X[:, t * H:(t + 1) * H]).then_inc(stored, 16)
            sp.wait_ge(stored, 16 * (B * NT // 2 + 1))

        @block.gpsimd
        def _(pool):
            pool.memset(ones[:, :], 0.0).then_inc(const_step, 1)
            pool.wait_ge(const_step, 1)
            pool.memset(ones[:, 3:4], 1.0).then_inc(ones_ready, 1)
            pool.memset(ROWS[0:K3, :], 0.0).then_inc(rows_zeroed, 1)
            pool.memset(identF[:, :], 0.0).then_inc(const_step, 1)
            pool.memset(fold[:, :], 0.0).then_inc(const_step, 1)
            pool.memset(qmask[:, :], 1.0).then_inc(const_step, 1)
            pool.memset(eps_col[:, :], EPS).then_inc(consts_done, 1)
            pool.memset(quad, 1.0).then_inc(const_step, 1)
            pool.wait_ge(const_step, 5)
            pool.affine_select(out=identF[:, :], in_=identF[:, :], compare_op=ALU.not_equal, fill=1.0,
                               base=0, pattern=[[-1, P]], channel_multiplier=1).then_inc(const_step, 1)
            pool.affine_select(out=qmask[:, :], in_=qmask[:, :], compare_op=ALU.is_ge, fill=0.0,
                               base=0, pattern=[[-32, 4]], channel_multiplier=1).then_inc(const_step, 1)
            pool.affine_select(out=quad, in_=quad, compare_op=ALU.is_ge, fill=0.0,
                               base=0, pattern=[[1, P]], channel_multiplier=-32).then_inc(const_step, 1)
            pool.wait_ge(const_step, 8)
            pool.affine_select(out=qmask[:, :], in_=qmask[:, :], compare_op=ALU.is_ge, fill=0.0,
                               base=31, pattern=[[32, 4]], channel_multiplier=-1).then_inc(const_step, 1)
            pool.affine_select(out=quad, in_=quad, compare_op=ALU.is_ge, fill=0.0,
                               base=31, pattern=[[-1, P]], channel_multiplier=32).then_inc(const_step, 1)
            for q in range(4):
                if q:
                    pool.wait_ge(const_step, 10 + q)
                pool.affine_select(out=fold[:, :], in_=fold[:, :], compare_op=ALU.not_equal, fill=1.0,
                                   base=-32 * q, pattern=[[-1, 32]], channel_multiplier=1).then_inc(const_step, 1)
            pool.wait_ge(const_step, 14)
            pool.memset(fence[:, :], 0.0).then_inc(consts_done, 1)

            def add_p(b):
                for j in range(NT):
                    if not (isinstance(b, int) and b == 0 and j < 2):
                        pool.wait_ge(sq_done, b * NT + j - 1)
                    pool.tensor_tensor(x2[:, j % 2, :], x_tile(b, j), Pb[:, bass.ds((b % 2) * H, H)],
                                       ALU.add).then_inc(x2_done, 1)

            pool.wait_ge(p_ready, 1)
            add_p(0)
            with pool.Fori(1, B) as b:
                pool.wait_ge(p_ready, b + 1)
                add_p(b)

        @block.scalar
        def _(act):
            act.preload_act_table_set("natural_log_exp_and_others")

            def rowsum(b, j):
                if j % (NT // 2) == 0:
                    act.wait_ge(x_landed[b][j // (NT // 2)], 16)
                if b or j:
                    act.wait_ge(rowsum_done, b * NT + j)
                act.activation(rowjunk[:, :], x_tile(b, j), ACT.Copy, scale=-1.0 / H,
                               accum_out=negx[:, bass.ds(b * NT + j, 1)]).then_inc(rowsum_done, 1)

            def r_copy(b):
                act.wait_ge(r_summed, b + 1)
                if b:
                    act.wait_ge(rt_psum, b)
                act.activation(RB[:, :], psB[:, 0:HALF], ACT.Copy).then_inc(r_copied, 1)

            def v_copy(b):
                act.wait_ge(v_done, b + 1)
                act.activation(Pb[:, bass.ds((b % 2) * H + HALF, QK)], psB[:, HALF:HALF + QK],
                               ACT.Copy).then_inc(v_copied, 1)

            def kk_sum(b):
                act.wait_ge(k_done, b + 1)
                if b >= 2:
                    act.wait_ge(x2_done, (b - 1) * NT)
                act.activation(Pb[:, bass.ds((b % 2) * H, QK)], psB[:, 0:QK], ACT.Square,
                               accum_out=st[:, 1:2]).then_inc(kk_summed, 1)

            def key_rms(b):
                act.wait_ge(row_step, ROW_STEPS * b + 2)
                act.activation(sc[1], sc[0], ACT.Ln).then_inc(row_act, 1)
                act.wait_ge(row_act, 4 * b + 1)
                act.activation(sc[2], sc[1], ACT.Exp, scale=-0.5).then_inc(row_act, 1)

            def softmax_exp(b):
                act.wait_ge(row_step, ROW_STEPS * b + 8)
                act.activation(sc[6], sc[5], ACT.Exp, accum_out=sc[7][:, 0:1]).then_inc(row_act, 2)

            def p_copy(b):
                act.wait_ge(pb_psum, 2 * (b + 1))
                act.wait_ge(pt_psum, b + 1)
                act.activation(Pb[:, bass.ds((b % 2) * H, H)], (psB if b else psA)[:, :], ACT.Copy,
                               accum_out=sumP[:, 0:1]).then_inc(p_ready, 1)

            def neg_mu(b):
                act.wait_ge(p_ready, b + 1)
                act.activation(sumP[:, 1:2], sumP[:, 0:1], ACT.Copy, scale=-1.0 / H).then_inc(nmu_step, 1)
                act.wait_ge(nmu_step, 2 * b + 1)
                act.wait_ge(rowsum_done, (b + 1) * NT)
                act.activation(negmu[:, bass.ds(b * NT, NT)], negx[:, bass.ds(b * NT, NT)], ACT.Identity,
                               bias=sumP[:, 1:2]).then_inc(nmu_step, 1)
                act.wait_ge(nmu_step, 2 * b + 2)

            def square(b, j):
                act.wait_ge(x2_done, b * NT + j + 1)
                act.activation(x2[:, j % 2, :], x2[:, j % 2, :], ACT.Square,
                               bias=negmu[:, bass.ds(b * NT + j, 1)],
                               accum_out=sqs[:, bass.ds(b * NT + j, 1)]).then_inc(sq_done, 1)

            def first_rstd(b, g):
                at = bass.ds(b * NT + g * G, G)
                act.wait_ge(sq_done, b * NT + (g + 1) * G)
                act.activation(r0[:, at], sqs[:, at], ACT.Ln, scale=1.0 / H, bias=eps_col[:, :]).then_inc(r0_step, 1)
                act.wait_ge(r0_step, 2 * (NG * b + g) + 1)
                act.activation(r0[:, at], r0[:, at], ACT.Exp, scale=-0.5).then_inc(r0_step, 1)

            def w_copy(m):
                WT = WkT if m < HC else WoT
                k = BLOCKS[m % HC]
                for h in range(2):
                    act.wait_ge(w_psum, 2 * m + h + 1)
                    act.activation(WT[:, 4 * h:4 * h + 4, k * P:(k + 1) * P],
                                   psA[:, h * HALF:(h + 1) * HALF].rearrange("p (c k) -> p c k", c=4),
                                   ACT.Copy).then_inc(w_act, 1)

            for j in range(NT // 2 + 1):
                rowsum(0, j)
            r_copy(0)
            for m in range(0, 2 * HC, 2):
                w_copy(m)
                if m < 6:
                    rowsum(0, NT // 2 + 1 + m // 2)
                if m == HC:
                    kk_sum(0)
                if m == HC + 4:
                    act.wait_ge(consts_done, N_CONST)
                    key_rms(0)
            softmax_exp(0)
            v_copy(0)
            p_copy(0)

            rowsum(1, 0)
            rowsum(1, 1)
            for t in range(B * NT):
                b, j = divmod(t, NT)
                if j == 0:
                    neg_mu(b)
                square(b, j)
                if j % G == G - 1:
                    first_rstd(b, j // G)
                for c in range(1, B):
                    k = t - BASE[c]
                    if k == 6 or (c == 1 and t == 0):
                        r_copy(c)
                    if k == 10:
                        kk_sum(c)
                    if k == 12:
                        v_copy(c)
                        key_rms(c)
                    if k == 13:
                        softmax_exp(c)
                    if k == 14:
                        p_copy(c)
                if t + NT + 2 < B * NT:
                    rowsum((t + NT + 2) // NT, (t + 2) % NT)

        @block.vector
        def _(dve):
            steps = [0]

            def const(ins):
                ins.then_inc(dconst, 1)
                steps[0] += 1
                dve.wait_ge(dconst, steps[0])

            dve.wait_ge(consts_done, N_CONST)
            const(dve.tensor_copy(identB[:, :], identF[:, :]))
            const(dve.memset(arow, 0.0))
            const(dve.memset(orow, 1.0))
            const(dve.memset(MC[:, :, :], 0.0))
            const(dve.memset(SM[:, :, :], 0.0))
            const(dve.memset(LT[:, :], 0.0))
            dve.memset(SM[:, :, ROW_ONE:ROW_ONE + 3], 1.0).then_inc(dconst, 1)
            steps[0] += 1
            dve.wait_ge(small_landed, 64)
            dve.tensor_tensor(x2[0:4, 1, 0:QK], x2[0:4, 1, 0:QK], x2[0:4, 1, QK:2 * QK], ALU.mult).then_inc(v_row, 1)
            dve.wait_ge(gb_psum, 1)
            const(dve.tensor_copy(GB[:, :, :], ps6[:, 0:2 * HC].rearrange("p (v c) -> p v c", v=2)))
            const(dve.tensor_copy(vv[:, :], ps6[:, QK:2 * QK]))
            const(dve.tensor_copy(gbp[:, 0, :, :], GB[:, :, :]))
            const(dve.tensor_tensor(pp[:, :, :], GB[:, :, :], gbp[:, 0, :, :], ALU.subtract))
            const(dve.tensor_copy(gbp[:, 1, :, :], pp[:, :, :]))
            const(dve.tensor_tensor(gbp[:, 2, :, :], pp[:, :, :], gbp[:, 1, :, :], ALU.subtract))

            def part_rows(v, at, reps):
                return (MC[:, :, at:at + 3 * reps].rearrange("p c (i j) -> p c i j", j=3),
                        gbp[:, :, v, :].rearrange("p j c -> p c j").unsqueeze(2).broadcast_to([P, HC, reps, 3]))

            o, i = part_rows(0, 0, 3)
            const(dve.tensor_copy(o, i))
            const(dve.memset(MC[:, :, ROW_ONE:ROW_ONE + 1], 1.0))
            dve.sem_inc(ma_ready, 1)

            def a_rows():
                dve.wait_ge(ra_psum, 1)
                const(dve.tensor_copy(RA, ps7[KR:2 * KR, :]))
                o, i = part_rows(0, ROW_M, 3)
                const(dve.tensor_copy(o, i))
                o, i = part_rows(1, ROW_ONE, 1)
                const(dve.tensor_copy(o, i))

            def rt_copy(b):
                dve.wait_ge(rt_psum, b + 1)
                src = psB[:, HALF:H].rearrange("p (c f u i) -> p c f u i", f=2, u=2, i=32)
                for f in range(2):
                    dst = rT[:, 4 * f:4 * f + 4, :].rearrange("p c (u i) -> p c u i", u=2)
                    dve.tensor_copy(dst, src[:, :, f, :, 0:16]).then_inc(rt_copied, 1)

            def score(b):
                dve.wait_ge(kk_summed, b + 1)
                dve.scalar_tensor_tensor(out=psB[:, 0:QK], in0=psB[:, 0:QK],
                                         scalar=1.0, in1=vv[:, :], op0=ALU.mult, op1=ALU.mult,
                                         accum_out=st[:, 0:1]).then_inc(kv_scored, 1)

            def row_ops(b):
                return lambda ins: ins.then_inc(row_step, 1), lambda n: dve.wait_ge(row_step, ROW_STEPS * b + n)

            def view8(ap):
                return ap.rearrange("o (u i) -> o u i", u=2)

            def row_a(b):
                done, after = row_ops(b)
                dve.wait_ge(rows_psum, b + 1)
                done(dve.tensor_copy(row, psum_rows))
                after(1)
                ss = row[:, 32:64].rearrange("o (u i) -> o u i", u=2)[:, :, 0:4]
                done(dve.tensor_scalar(view8(sc[0]), ss, 1.0 / H, EPS, ALU.mult, ALU.add))

            def row_b(b):
                done, after = row_ops(b)
                s = row[:, 0:32].rearrange("o (u i) -> o u i", u=2)[:, :, 0:4]
                dve.wait_ge(row_act, 4 * b + 2)
                done(dve.scalar_tensor_tensor(out=sc[3], in0=sc[0], scalar=-0.5, in1=sc[2],
                                              op0=ALU.mult, op1=ALU.mult))
                after(3)
                done(dve.tensor_tensor(sc[4], sc[3], sc[2], ALU.mult))
                after(4)
                done(dve.scalar_tensor_tensor(out=sc[1], in0=sc[4], scalar=1.5, in1=sc[2],
                                              op0=ALU.add, op1=ALU.mult))
                after(5)
                done(dve.tensor_tensor(view8(sc[3]), s, view8(sc[1]), ALU.mult))
                after(6)
                done(dve.reduce_max(sc[4][:, 0:1], sc[3], AX.X))
                after(7)
                done(dve.tensor_scalar(sc[5], sc[3], sc[4][:, 0:1], None, ALU.subtract))

            def row_c(b):
                done, after = row_ops(b)
                dve.wait_ge(row_act, 4 * b + 4)
                done(dve.reciprocal(sc[7][:, 1:2], sc[7][:, 0:1]))
                after(9)
                dst = arow.rearrange("o (q u i) -> o q u i", q=4, u=2)[:, :, :, 0:4]
                src = view8(sc[6]).unsqueeze(1).broadcast_to([1, 4, 2, 4])
                done(dve.tensor_scalar(dst, src, sc[7][:, 1:2], None, ALU.mult))

            def col_a(b):
                done, after = row_ops(b)
                dve.wait_ge(acol_psum, b + 1)
                done(dve.tensor_copy(attn[:, :], psum_attn))
                done(dve.tensor_tensor(acol[:, :], qmask[:, :], psum_attn[:, 0:4], ALU.mult))

            def col_b(b):
                done, after = row_ops(b)
                dve.wait_ge(pt_psum, b + 1)
                pt = psum_pt.rearrange("p (s q) -> p q s", s=2)
                kc = lambda ap: ap.rearrange("p (q s) -> p q s", s=2)
                done(dve.tensor_copy(kc(pp[:, 0, :]), pt))
                done(dve.tensor_tensor(kc(pp[:, 1, :]), pt, kc(GB[:, 0, :]), ALU.mult))
                after(14)
                done(dve.tensor_copy(ppp[:, 0, :, :], pp[:, :, :]))
                after(15)
                done(dve.tensor_tensor(pd[:, :, :], pp[:, :, :], ppp[:, 0, :, :], ALU.subtract))
                after(16)
                done(dve.tensor_copy(ppp[:, 1, :, :], pd[:, :, :]))
                after(17)
                done(dve.tensor_tensor(ppp[:, 2, :, :], pd[:, :, :], ppp[:, 1, :, :], ALU.subtract))
                after(18)
                part = lambda v: ppp[:, :, v, :].rearrange("p j c -> p c j")
                done(dve.tensor_copy(MC[:, :, ROW_P:ROW_P + 3], part(0)))
                done(dve.tensor_copy(MC[:, :, 0:9].rearrange("p c (i j) -> p c i j", j=3),
                                     part(1).unsqueeze(2).broadcast_to([P, HC, 3, 3])))

            def rc_copy(b, t=None):
                dve.wait_ge(rc_psum, b + 1)
                if t is not None:
                    dve.wait_ge(c_ready, t + 1)
                c = C_AT[b % 2]
                dve.tensor_copy(ROWS[c:c + KR, H:2 * H], ps7[c:c + KR, :]).then_inc(rc_ready, 1)

            def stats(b, g):
                gi = NG * b + g
                at = bass.ds(b * NT + g * G, G)
                done = lambda ins: ins.then_inc(stat_step, 1)
                after = lambda n: dve.wait_ge(stat_step, STAT_STEPS * gi + n)
                dve.wait_ge(r0_step, 2 * (gi + 1))
                done(dve.tensor_scalar(var[:, :], sqs[:, at], 1.0 / H, EPS, ALU.mult, ALU.add))
                after(1)
                done(dve.scalar_tensor_tensor(out=nt1[:, :], in0=var[:, :], scalar=-0.5, in1=r0[:, at],
                                              op0=ALU.mult, op1=ALU.mult))
                after(2)
                done(dve.tensor_tensor(nt2[:, :], nt1[:, :], r0[:, at], ALU.mult))
                after(3)
                done(dve.scalar_tensor_tensor(out=RM[:, :, 0], in0=nt2[:, :], scalar=1.5, in1=r0[:, at],
                                              op0=ALU.add, op1=ALU.mult))
                after(4)
                done(dve.tensor_tensor(RM[:, :, 1], RM[:, :, 0], negmu[:, at], ALU.mult))
                after(5)
                part = lambda i: SM[:, :, 0:18].rearrange("p t (v i j) -> p t v i j", i=3, j=3)[:, :, :, i, :]
                rep = lambda ap: ap.unsqueeze(3).broadcast_to([P, G, 2, 3])
                done(dve.tensor_copy(part(0), rep(RM[:, :, :])))
                after(6)
                done(dve.tensor_tensor(RMd[:, :, :], RM[:, :, :], part(0)[:, :, :, 0], ALU.subtract))
                after(7)
                done(dve.tensor_copy(part(1), rep(RMd[:, :, :])))
                after(8)
                done(dve.tensor_tensor(part(2), rep(RMd[:, :, :]), part(1), ALU.subtract))

            def lt_copy(b, g):
                dve.wait_ge(lt_psum, NG * b + g + 1)
                if b or g:
                    dve.wait_ge(c_ready, b * NT + g * G)
                if b % 2 == 0:
                    if b and g == 0:
                        dve.memset(LT[2 * KR:K3, :], 0.0)
                    dve.tensor_copy(LT[0:2 * KR, :], ps6h[0:2 * KR, 0:G * P]).then_inc(lt_ready, 1)
                else:
                    if g == 0:
                        dve.memset(LT[0:KR, :], 0.0)
                    dve.tensor_copy(LT[KR:2 * KR, :], ps6h[KR:2 * KR, 0:G * P])
                    dve.tensor_copy(LT[2 * KR:K3, :], ps6h[2 * KR:K3, 0:G * P]).then_inc(lt_ready, 1)

            def mult(b, j):
                dve.wait_ge(a_ready, b * NT + j + 1)
                dve.tensor_tensor(x_tile(b, j), x_tile(b, j), psA[:, :], ALU.mult).then_inc(mult_done, 1)

            def add(b, j):
                dve.wait_ge(c_ready, b * NT + j + 1)
                dve.wait_ge(mult_done, b * NT + j + 1)
                dve.tensor_tensor(x_tile(b, j), x_tile(b, j), psC[:, :], ALU.add).then_inc(final_done, 1)

            def w_copy(m):
                WT = WkT if m < HC else WoT
                k = BLOCKS[m % HC]
                for h in range(2):
                    dve.wait_ge(w_psum, 2 * m + h + 1)
                    dve.tensor_copy(WT[:, 4 * h:4 * h + 4, k * P:(k + 1) * P],
                                    psC[:, h * HALF:(h + 1) * HALF].rearrange("p (c k) -> p c k", c=4)).then_inc(w_dve, 1)

            rt_copy(0)
            for m in range(1, 2 * HC, 2):
                w_copy(m)
                if m == 1:
                    a_rows()
                if m == HC + 1:
                    score(0)
                if m == HC + 3:
                    row_a(0)
                if m == HC + 5:
                    row_b(0)
            row_c(0)
            col_a(0)
            col_b(0)
            rc_copy(0)
            rt_copy(1)
            score(1)
            row_a(1)
            stats(0, 0)
            lt_copy(0, 0)

            for t in range(B * NT):
                b, j = divmod(t, NT)
                if t % G == G - 1 and t + 1 < B * NT:
                    stats(*divmod((t + 1) // G, NG))
                mult(b, j)
                if t % G == G - 1 and t + 1 < B * NT:
                    lt_copy(*divmod((t + 1) // G, NG))
                for c in range(1, B):
                    k = t - BASE[c]
                    if k == 3:
                        rt_copy(c)
                    if k == 5:
                        score(c)
                    if k == 6:
                        row_a(c)
                    if k == 7:
                        row_b(c)
                    if k == 8:
                        row_c(c)
                    if k == 12:
                        rc_copy(c, t)
                add(b, j)
                for c in range(1, B):
                    k = t - BASE[c]
                    if k == 8:
                        col_a(c)
                    if k == 10:
                        col_b(c)

        @block.tensor
        def _(pe):
            mm = nc.tensor.matmul

            def sums(b, half):
                pe.wait_ge(x_landed[b][half], 16)
                for i in range(half * NT // 4, (half + 1) * NT // 4):
                    for f in range(2):
                        for u in range(2):
                            q = 2 * f + u
                            at = (b * NT + 2 * i + u) * H + f * HALF
                            last = mm(psB[32 * q:32 * q + 32, 0:HALF], ones[:, 3 - i:35 - i],
                                      X[:, at:at + HALF], start=(i == 0), stop=(i == NT // 2 - 1))
                if half:
                    last.then_inc(r_summed, 1)

            def sums_t(b):
                pe.wait_ge(r_copied, b + 1)
                if b >= 2:
                    pe.wait_ge(p_ready, b)
                for c in range(4):
                    last = nc.tensor.transpose(psB[:, HALF + c * P:HALF + (c + 1) * P],
                                               RB[:, c * P:(c + 1) * P], identF[:, :])
                last.then_inc(rt_psum, 1)

            def times_w(at, WT, sub, n, done=None):
                for c in range(HC):
                    for q in range(4):
                        k = q * QK + sub * P
                        last = mm(psB[32 * q:32 * q + 32, at + sub * P:at + sub * P + n], rT[:, c, :],
                                  WT[:, c, k:k + n], start=(c == 0), stop=(c == HC - 1))
                if done is not None:
                    last.then_inc(done, 1)

            def keys(b, sub):
                pe.wait_ge(rt_copied, 2 * (b + 1))
                times_w(0, WkT, sub, P, k_done if sub else None)

            def values(b, sub):
                times_w(HALF, WoT, sub, P, v_done if sub else None)

            def rows(b):
                pe.wait_ge(kv_scored, b + 1)
                pe.wait_ge(kk_summed, b + 1)
                if b:
                    pe.wait_ge(rc_ready, b)
                mm(psum_rows[:, 0:32], st[:, 0:1], fold[:, :], start=True, stop=True)
                mm(psum_rows[:, 32:64], st[:, 1:2], fold[:, :], start=True, stop=True).then_inc(rows_psum, 1)

            def attn_col(b):
                pe.wait_ge(row_step, ROW_STEPS * b + 10)
                mm(psum_attn, arow, orow, start=True, stop=True).then_inc(acol_psum, 1)

            def p_rows(b):
                pe.wait_ge(row_step, ROW_STEPS * b + 12)
                pe.wait_ge(v_copied, b + 1)
                if b and b + 1 < B:
                    pe.wait_ge(r_copied, b + 2)
                at = (b % 2) * H + HALF
                for q in (0, 2, 1, 3):
                    if q == 1:
                        pe.wait_ge(p_halves, 2 * (b + 1))
                    mm((psB if b else psA)[:, q * QK:(q + 1) * QK], attn[32 * q:32 * q + 32, :],
                       Pb[32 * q:32 * q + 32, at:at + QK], start=True, stop=True).then_inc(
                        pb_psum if q % 2 else p_halves, 1)
                for s in range(2):
                    last = mm(psum_pt[:, 4 * s:4 * s + 4], Pb[:, at + s * P:at + (s + 1) * P], acol[:, :],
                              start=True, stop=True)
                last.then_inc(pt_psum, 1)

            def part_rows(lo, done):
                for c in range(HC):
                    last = nc.tensor.transpose(ps7[lo:lo + KR, c * P:(c + 1) * P], MC[:, c, :], identB[:, :])
                last.then_inc(done, 1)

            def c_rows(b):
                pe.wait_ge(row_step, ROW_STEPS * (b + 1))
                part_rows(C_AT[b % 2], rc_psum)

            def stat_rows(b, g):
                gi = NG * b + g
                pe.wait_ge(stat_step, STAT_STEPS * (gi + 1))
                for t in range(G):
                    for lo in (KR, C_AT[b % 2]):
                        last = nc.tensor.transpose(ps6h[lo:lo + KR, t * P:(t + 1) * P], SM[:, t, :], identB[:, :])
                last.then_inc(lt_psum, 1)

            def outer(b, j, ps, at, ready, freed):
                t = b * NT + j
                pe.wait_ge(lt_ready, NG * b + j // G + 1)
                if t:
                    pe.wait_ge(freed, t)
                for f in range(2):
                    last = mm(ps[:, f * HALF:(f + 1) * HALF], LT[:, (j % G) * P:(j % G + 1) * P],
                              ROWS[0:K3, at + f * HALF:at + (f + 1) * HALF], start=True, stop=True)
                last.then_inc(ready, 1)

            def a_tile(b, j):
                outer(b, j, psA, 0, a_ready, mult_done)

            def c_tile(b, j):
                outer(b, j, psC, H, c_ready, final_done)

            def w_block(m):
                stage, landed = (2, wk_landed) if m < HC else (3, wo_landed)
                k = BLOCKS[m % HC]
                if m % 2 == 0:
                    pe.wait_ge(landed[m % HC // 2], 16)
                ps, freed = (psA, w_act) if m % 2 == 0 else (psC, w_dve)
                for h in range(2):
                    if m >= 2:
                        pe.wait_ge(freed, 2 * (m // 2 - 1) + h + 1)
                    for c in range(4 * h, 4 * h + 4):
                        at = (stage * NT + k) * H + c * P
                        last = nc.tensor.transpose(ps[:, c * P:(c + 1) * P], X[:, at:at + P], identF[:, :])
                    last.then_inc(w_psum, 1)

            def w_copied(m):
                pe.wait_ge(w_act, m)
                pe.wait_ge(w_dve, m)

            pe.wait_ge(rows_zeroed, 1)
            for _ in range(14):
                mm(ps6[:, :], ROWS[0:K3, 0:P], ROWS[0:K3, 0:HALF], start=True, stop=True)
            pe.wait_ge(ones_ready, 1)
            sums(0, 0)
            pe.wait_ge(consts_done, N_CONST)
            pe.wait_ge(small_landed, 64)
            nc.tensor.transpose(ps6[:, 0:2 * HC], x2[0:2 * HC, 0, 0:P], identF[0:2 * HC, 0:2 * HC])
            pe.wait_ge(v_row, 1)
            mm(ps6[:, QK:2 * QK], quad, x2[0:4, 1, 0:QK], start=True, stop=True).then_inc(gb_psum, 1)
            sums(0, 1)
            sums_t(0)
            w_block(0)
            w_block(1)
            pe.wait_ge(ma_ready, 1)
            part_rows(KR, ra_psum)
            w_block(2)
            w_block(3)
            w_copied(4)
            keys(0, 0)
            for m in range(4, HC):
                w_block(m)
            w_copied(HC)
            keys(0, 1)
            for m in range(HC, HC + 4):
                w_block(m)
            rows(0)
            w_block(HC + 4)
            w_block(HC + 5)
            values(0, 0)
            w_block(HC + 6)
            w_block(HC + 7)
            attn_col(0)
            w_copied(2 * HC)
            values(0, 1)
            p_rows(0)
            c_rows(0)
            sums(1, 0)
            sums(1, 1)
            sums_t(1)
            keys(1, 0)
            keys(1, 1)
            values(1, 0)
            rows(1)
            values(1, 1)
            stat_rows(0, 0)

            for t in range(B * NT):
                b, j = divmod(t, NT)
                a_tile(b, j)
                for c in range(1, B):
                    if t - BASE[c] == 3:
                        sums_t(c)
                    if t - BASE[c] == 12:
                        c_rows(c)
                c_tile(b, j)
                if t % G == G - 1 and t + 1 < B * NT:
                    stat_rows(*divmod((t + 1) // G, NG))
                for c in range(1, B):
                    k = t - BASE[c]
                    if k == 3:
                        keys(c, 0)
                    if k == 4:
                        keys(c, 1)
                    if k == 5:
                        values(c, 0)
                        rows(c)
                    if k == 6:
                        values(c, 1)
                    if k == 8:
                        attn_col(c)
                    if k in (7, 8) and c + 1 < B:
                        sums(c + 1, k - 7)
                    if k == 9:
                        p_rows(c)


_INS = ['x', 'cond_2048', 'L0_cond_rms_weight', 'L0_cond_Wk', 'L0_cond_Wo', 'L0_cond_ln_gamma', 'L0_cond_ln_beta']


def kernel(**inputs):
    import numpy as _np
    import concourse.bacc as _bacc
    from concourse.bass_utils import run_bass_kernel_spmd as _run

    nc = _bacc.Bacc("TRN2", target_bir_lowering=False, num_devices=1, dynamic_dma_scratch_size=1024)
    arrays, args = {}, []
    for name in _INS:
        a = _np.ascontiguousarray(inputs[name])
        arrays[f"in_{name}_dram"] = a
        args.append(nc.dram_tensor(f"in_{name}_dram", a.shape, mybir.dt.from_np(a.dtype), kind="ExternalInput").ap())
    x = inputs['x']
    args.append(nc.dram_tensor("out_0_dram", x.shape, F32, kind="ExternalOutput").ap())
    bass_block_attention_residual_norm_kernel(nc, *args)
    r = _run(nc, [arrays], core_ids=[0])
    return r.results[0]["out_0_dram"]
```

```python
import concourse.bass as bass
from concourse import mybir
from contextlib import ExitStack

F32 = mybir.dt.float32
BF16 = mybir.dt.bfloat16
ALU = mybir.AluOpType
ACT = mybir.ActivationFunctionType
AX = mybir.AxisListType

LAYER = 1
NUM_BLOCKS = 8
EPS = 1e-6


def bass_block_attention_residual_norm_kernel(
    nc: bass.Bass,
    x: bass.AP,
    cond: bass.AP,
    rms_weight: bass.AP,
    Wk: bass.AP,
    Wo: bass.AP,
    gamma: bass.AP,
    beta: bass.AP,
    out: bass.AP,
):
    B, S, H = x.shape
    P = 128
    NT = S // P
    HC = H // P
    HALF = H // 2
    QK = H // 4
    G = 4
    NG = NT // G
    KR = 32
    ROW_M, ROW_ONE = 9, 18
    assert S // NUM_BLOCKS == P and NT == 8 and HC == 8 and HALF == 512 and B == 4

    x_dram = x.rearrange("b (n p) h -> b p n h", p=P)
    out_dram = out.rearrange("b (n p) h -> p (b n) h", p=P)
    BLOCKS = [0, 2, 4, 6, 1, 3, 5, 7]
    wk_dram = Wk.rearrange("(k p) h -> p k h", p=P)
    wo_dram = Wo.rearrange("(k p) h -> p k h", p=P)

    with ExitStack() as ctx:
        def sb(name, shape, dt=F32):
            return ctx.enter_context(nc.sbuf_tensor(name, shape, dt))

        def pb(name, shape, dt=F32):
            return ctx.enter_context(nc.psum_tensor(name, shape, dt))

        def sem(name):
            return ctx.enter_context(nc.semaphore(name))

        X = sb("X", [P, B * NT * H])
        WkT = sb("WkT", [P, HC, H])
        WoT = sb("WoT", [P, HC, H])
        Pb = sb("Pb", [P, 2 * H])
        x2 = sb("x2", [P, 2, H])
        K3 = 3 * KR
        ROWS = sb("ROWS", [P, 2 * H], BF16)
        RA = ROWS[KR:2 * KR, 0:H]
        C_AT = (0, 2 * KR)
        rT = sb("rT", [P, HC, 32])
        RB = sb("RB", [P, HALF])
        LT = sb("LT", [K3, NG, G * P], BF16)
        identF = sb("identF", [P, P])
        identB = sb("identB", [P, P], BF16)
        MC = sb("MC", [P, HC, KR], BF16)
        rowjunk = sb("rowjunk", [P, H], BF16)
        vv = sb("vv", [P, QK])
        fold = sb("fold", [P, 32])
        ones = sb("ones", [P, 35])
        qmask = sb("qmask", [P, 4])
        quad = WoT[0:4, 0, 0:P]
        attn = sb("attn", [P, P])
        GB = sb("GB", [P, 2, HC])
        gbp = sb("gbp", [P, 3, 2, HC], BF16)
        pp = sb("pp", [P, 2, HC])
        pd = sb("pd", [P, HC])
        ppp = sb("ppp", [P, 3, HC], BF16)
        eps_col = sb("eps_col", [P, 1])
        fence = sb("fence", [1, 1])
        st = sb("st", [P, 2])
        sumP = sb("sumP", [P, 2])
        negx = sb("negx", [P, B * NT])
        negmu = sb("negmu", [P, B * NT])
        sqs = sb("sqs", [P, B * NT])
        r0 = sb("r0", [P, B * NT])
        var = sb("var", [P, G])
        nt1 = sb("nt1", [P, G])
        nt2 = sb("nt2", [P, G])
        RM = sb("RM", [P, G, 2])
        RMd = sb("RMd", [P, G, 2])
        SM = sb("SM", [P, G, KR], BF16)
        spare = ROWS[K3:K3 + 1, 0:H].bitcast(F32)
        arow = spare[:, 0:P]
        orow = spare[:, P:2 * P]
        row = spare[:, 2 * P:2 * P + 64]
        sc = [spare[:, 3 * P + 8 * i:3 * P + 8 * (i + 1)] for i in range(8)]
        acol = sb("acol", [P, 4])

        psA = pb("psA", [P, H])
        psC = pb("psC", [P, H])
        psB = pb("psB", [P, H])
        ps6 = pb("ps6", [P, HALF])
        ps7 = pb("ps7", [P, H], BF16)
        ps6h = ps6[:, :].bitcast(BF16)
        ps7f = ps7[:, :].bitcast(F32)
        psum_attn, psum_rows, psum_pt = ps7f[:, 0:P], ps7f[K3:K3 + 1, P:P + 64], ps7f[:, P + 64:P + 64 + HC]

        x_landed = [[sem(f"x_landed{b}_{f}") for f in range(2)] for b in range(B)]
        wk_landed = [sem(f"wk_landed{m}") for m in range(4)]
        wo_landed = [sem(f"wo_landed{m}") for m in range(4)]
        small_landed = sem("small_landed")
        stored = sem("stored")
        consts_done = sem("consts_done")
        const_step = sem("const_step")
        dconst = sem("dconst")
        gb_psum = sem("gb_psum")
        v_row = sem("v_row")
        ma_ready = sem("ma_ready")
        ra_psum = sem("ra_psum")
        w_psum = sem("w_psum")
        w_act = sem("w_act")
        w_dve = sem("w_dve")
        r_summed = sem("r_summed")
        r_copied = sem("r_copied")
        rt_psum = sem("rt_psum")
        rt_copied = sem("rt_copied")
        k_done = sem("k_done")
        v_done = sem("v_done")
        v_copied = sem("v_copied")
        kv_scored = sem("kv_scored")
        kk_summed = sem("kk_summed")
        rows_psum = sem("rows_psum")
        row_step = sem("row_step")
        row_act = sem("row_act")
        acol_psum = sem("acol_psum")
        pt_psum = sem("pt_psum")
        rc_psum = sem("rc_psum")
        rc_ready = sem("rc_ready")
        ones_ready = sem("ones_ready")
        rows_zeroed = sem("rows_zeroed")
        pb_psum = sem("pb_psum")
        p_halves = sem("p_halves")
        p_ready = sem("p_ready")
        nmu_step = sem("nmu_step")
        rowsum_done = sem("rowsum_done")
        x2_done = sem("x2_done")
        sq_done = sem("sq_done")
        r0_step = sem("r0_step")
        stat_step = sem("stat_step")
        lt_psum = sem("lt_psum")
        lt_ready = sem("lt_ready")
        a_ready = sem("a_ready")
        c_ready = sem("c_ready")
        mult_done = sem("mult_done")
        final_done = sem("final_done")

        N_CONST = 2
        ROW_STEPS = 18
        STAT_STEPS = 10

        START = {1: -10, 2: 4, 3: 20}
        TE = dict(sums_t=-1, keys=1, values=6, rows=8, sums=8, attn=11, p_rows=12, c_rows=17)
        VE = dict(rt_copy=-1, score=6, row_a=7, row_b=8, row_c=9, col_a=10, col_b=15, rc_copy=18)
        R_AT = {1: 0, 2: 4, 3: 13}
        KK_AT = {1: 3, 2: 10, 3: 18}
        RMS_AT = {1: 3, 2: 11, 3: 20}
        EXP_AT = {1: 3, 2: 13, 3: 20}
        P_AT = {1: 6, 2: 14, 3: 22}
        NO_SUM, TWO_SUMS = (0, 4), (8, 8)

        block = ctx.enter_context(nc.Block())

        def x_tile(b, j, lo=0, n=H):
            return X[:, bass.ds((b * NT + j) * H + lo, n)]

        @block.sync
        def _(sp):
            def stage(b):
                return X[:, b * NT * H:(b + 1) * NT * H].rearrange("p (n h) -> p n h", h=H)

            def load_x(b, f):
                n = slice(f * NT // 2, (f + 1) * NT // 2)
                sp.dma_start(stage(b)[:, n, :], x_dram[b][:, n, :]).then_inc(x_landed[b][f], 16)

            load_x(0, 0)
            for at, src in ((0, gamma), (HC, beta)):
                sp.dma_start(x2[at:at + HC, 0, 0:P], src.rearrange("(c p) -> c p", p=P)).then_inc(small_landed, 16)
            for at, src in ((0, cond[LAYER, :]), (QK, rms_weight)):
                sp.dma_start(x2[0:4, 1, at:at + QK], src.rearrange("(q k) -> q k", q=4)).then_inc(small_landed, 16)
            load_x(0, 1)
            for dram, at, landed in ((wk_dram, 2, wk_landed), (wo_dram, 3, wo_landed)):
                for m in range(4):
                    k0 = BLOCKS[2 * m]
                    sp.dma_start(stage(at)[:, k0:k0 + 3:2, :], dram[:, k0:k0 + 3:2, :]).then_inc(landed[m], 16)
            load_x(1, 0)
            load_x(1, 1)
            sp.wait_ge(w_psum, 2 * HC)
            load_x(2, 0)
            load_x(2, 1)
            sp.wait_ge(w_psum, 4 * HC)
            load_x(3, 0)
            load_x(3, 1)
            with sp.Fori(0, B * NT // 2 - 1) as i:
                sp.wait_ge(final_done, 2 * i + 2)
                sp.dma_start(out_dram[:, bass.ds(2 * i, 2), :],
                             X[:, bass.ds(2 * i * H, 2 * H)].rearrange("p (n h) -> p n h", h=H)).then_inc(stored, 16)
            for t in range(B * NT - 2, B * NT):
                sp.wait_ge(final_done, t + 1)
                sp.dma_start(out_dram[:, t, :], X[:, t * H:(t + 1) * H]).then_inc(stored, 16)
            sp.wait_ge(stored, 16 * (B * NT // 2 + 1))

        @block.gpsimd
        def _(pool):
            pool.memset(ones[:, :], 0.0).then_inc(const_step, 1)
            pool.wait_ge(const_step, 1)
            pool.memset(ones[:, 3:4], 1.0).then_inc(ones_ready, 1)
            pool.memset(ROWS[0:K3, :], 0.0).then_inc(rows_zeroed, 1)
            pool.memset(identF[:, :], 0.0).then_inc(const_step, 1)
            pool.memset(fold[:, :], 0.0).then_inc(const_step, 1)
            pool.memset(qmask[:, :], 1.0).then_inc(const_step, 1)
            pool.memset(eps_col[:, :], EPS).then_inc(consts_done, 1)
            pool.memset(quad, 1.0).then_inc(const_step, 1)
            pool.wait_ge(const_step, 5)
            pool.affine_select(out=identF[:, :], in_=identF[:, :], compare_op=ALU.not_equal, fill=1.0,
                               base=0, pattern=[[-1, P]], channel_multiplier=1).then_inc(const_step, 1)
            pool.affine_select(out=qmask[:, :], in_=qmask[:, :], compare_op=ALU.is_ge, fill=0.0,
                               base=0, pattern=[[-32, 4]], channel_multiplier=1).then_inc(const_step, 1)
            pool.affine_select(out=quad, in_=quad, compare_op=ALU.is_ge, fill=0.0,
                               base=0, pattern=[[1, P]], channel_multiplier=-32).then_inc(const_step, 1)
            pool.wait_ge(const_step, 8)
            pool.affine_select(out=qmask[:, :], in_=qmask[:, :], compare_op=ALU.is_ge, fill=0.0,
                               base=31, pattern=[[32, 4]], channel_multiplier=-1).then_inc(const_step, 1)
            pool.affine_select(out=quad, in_=quad, compare_op=ALU.is_ge, fill=0.0,
                               base=31, pattern=[[-1, P]], channel_multiplier=32).then_inc(const_step, 1)
            for q in range(4):
                if q:
                    pool.wait_ge(const_step, 10 + q)
                pool.affine_select(out=fold[:, :], in_=fold[:, :], compare_op=ALU.not_equal, fill=1.0,
                                   base=-32 * q, pattern=[[-1, 32]], channel_multiplier=1).then_inc(const_step, 1)
            pool.wait_ge(const_step, 14)
            pool.memset(fence[:, :], 0.0).then_inc(consts_done, 1)

            def add_p(t):
                if t >= 2:
                    pool.wait_ge(sq_done, t - 1)
                pool.tensor_tensor(x2[:, t % 2, :], X[:, t * H:(t + 1) * H],
                                   Pb[:, (t // NT % 2) * H:(t // NT % 2 + 1) * H], ALU.add).then_inc(x2_done, 1)

            def stats(g):
                at = slice(g * G, (g + 1) * G)
                done = lambda ins: ins.then_inc(stat_step, 1)
                after = lambda n: pool.wait_ge(stat_step, STAT_STEPS * g + n)
                pool.wait_ge(r0_step, 2 * (g + 1))
                if g:
                    after(0)
                done(pool.tensor_scalar(var[:, :], sqs[:, at], 1.0 / H, EPS, ALU.mult, ALU.add))
                after(1)
                done(pool.tensor_tensor(nt1[:, :], var[:, :], r0[:, at], ALU.mult))
                after(2)
                done(pool.tensor_tensor(nt2[:, :], nt1[:, :], r0[:, at], ALU.mult))
                after(3)
                done(pool.tensor_scalar(nt1[:, :], nt2[:, :], -0.5, 1.5, ALU.mult, ALU.add))
                after(4)
                done(pool.tensor_tensor(RM[:, :, 0], nt1[:, :], r0[:, at], ALU.mult))
                after(5)
                done(pool.tensor_tensor(RM[:, :, 1], RM[:, :, 0], negmu[:, at], ALU.mult))
                after(6)
                if g:
                    pool.wait_ge(lt_psum, g)
                part = lambda i: SM[:, :, 0:18].rearrange("p t (v i j) -> p t v i j", i=3, j=3)[:, :, :, i, :]
                rep = lambda ap: ap.unsqueeze(3).broadcast_to([P, G, 2, 3])
                done(pool.tensor_copy(part(0), rep(RM[:, :, :])))
                after(7)
                done(pool.tensor_tensor(RMd[:, :, :], RM[:, :, :], part(0)[:, :, :, 0], ALU.subtract))
                after(8)
                done(pool.tensor_copy(part(1), rep(RMd[:, :, :])))
                after(9)
                done(pool.tensor_tensor(part(2), rep(RMd[:, :, :]), part(1), ALU.subtract))

            for t in range(B * NT):
                if t % NT == 0:
                    pool.wait_ge(p_ready, t // NT + 1)
                add_p(t)
                if t == G - 1:
                    stats(0)
                if t > G and t % G == 0:
                    stats(t // G - 1)
            stats(B * NT // G - 1)

        @block.scalar
        def _(act):
            act.preload_act_table_set("natural_log_exp_and_others")

            def rowsum(b, j):
                if j % (NT // 2) == 0:
                    act.wait_ge(x_landed[b][j // (NT // 2)], 16)
                if b or j:
                    act.wait_ge(rowsum_done, b * NT + j)
                act.activation(rowjunk[:, :], x_tile(b, j), ACT.Copy, scale=-1.0 / H,
                               accum_out=negx[:, bass.ds(b * NT + j, 1)]).then_inc(rowsum_done, 1)

            def r_copy(b):
                act.wait_ge(r_summed, b + 1)
                if b:
                    act.wait_ge(rt_psum, b)
                act.activation(RB[:, :], psB[:, 0:HALF], ACT.Copy).then_inc(r_copied, 1)

            def v_copy(b):
                act.wait_ge(v_done, b + 1)
                act.activation(Pb[:, bass.ds((b % 2) * H + HALF, QK)], psB[:, HALF:HALF + QK],
                               ACT.Copy).then_inc(v_copied, 1)

            def kk_sum(b):
                act.wait_ge(k_done, b + 1)
                if b >= 2:
                    act.wait_ge(x2_done, (b - 1) * NT)
                act.activation(Pb[:, bass.ds((b % 2) * H, QK)], psB[:, 0:QK], ACT.Square,
                               accum_out=st[:, 1:2]).then_inc(kk_summed, 1)

            def key_rms(b):
                act.wait_ge(row_step, ROW_STEPS * b + 2)
                act.activation(sc[1], sc[0], ACT.Ln).then_inc(row_act, 1)
                act.wait_ge(row_act, 4 * b + 1)
                act.activation(sc[2], sc[1], ACT.Exp, scale=-0.5).then_inc(row_act, 1)

            def softmax_exp(b):
                act.wait_ge(row_step, ROW_STEPS * b + 8)
                act.activation(sc[6], sc[5], ACT.Exp, accum_out=sc[7][:, 0:1]).then_inc(row_act, 2)

            def p_copy(b):
                act.wait_ge(pb_psum, 2 * (b + 1))
                act.wait_ge(pt_psum, b + 1)
                act.activation(Pb[:, bass.ds((b % 2) * H, H)], (psB if b else psA)[:, :], ACT.Copy,
                               accum_out=sumP[:, 0:1]).then_inc(p_ready, 1)

            def neg_mu(b):
                act.wait_ge(p_ready, b + 1)
                act.activation(sumP[:, 1:2], sumP[:, 0:1], ACT.Copy, scale=-1.0 / H).then_inc(nmu_step, 1)
                act.wait_ge(nmu_step, 2 * b + 1)
                act.wait_ge(rowsum_done, (b + 1) * NT)
                act.activation(negmu[:, bass.ds(b * NT, NT)], negx[:, bass.ds(b * NT, NT)], ACT.Identity,
                               bias=sumP[:, 1:2]).then_inc(nmu_step, 1)
                act.wait_ge(nmu_step, 2 * b + 2)

            def square(b, j):
                act.wait_ge(x2_done, b * NT + j + 1)
                act.activation(x2[:, j % 2, :], x2[:, j % 2, :], ACT.Square,
                               bias=negmu[:, bass.ds(b * NT + j, 1)],
                               accum_out=sqs[:, bass.ds(b * NT + j, 1)]).then_inc(sq_done, 1)

            def first_rstd(b, g):
                at = bass.ds(b * NT + g * G, G)
                act.wait_ge(sq_done, b * NT + (g + 1) * G)
                act.activation(r0[:, at], sqs[:, at], ACT.Ln, scale=1.0 / H, bias=eps_col[:, :]).then_inc(r0_step, 1)
                act.wait_ge(r0_step, 2 * (NG * b + g) + 1)
                act.activation(r0[:, at], r0[:, at], ACT.Exp, scale=-0.5).then_inc(r0_step, 1)

            def w_copy(m):
                WT = WkT if m < HC else WoT
                k = BLOCKS[m % HC]
                for h in range(2):
                    act.wait_ge(w_psum, 2 * m + h + 1)
                    act.activation(WT[:, 4 * h:4 * h + 4, k * P:(k + 1) * P],
                                   psA[:, h * HALF:(h + 1) * HALF].rearrange("p (c k) -> p c k", c=4),
                                   ACT.Copy).then_inc(w_act, 1)

            for j in range(NT // 2 + 1):
                rowsum(0, j)
            r_copy(0)
            for m in range(0, 2 * HC, 2):
                w_copy(m)
                if m < 6:
                    rowsum(0, NT // 2 + 1 + m // 2)
                if m == HC + 2:
                    kk_sum(0)
                if m == HC + 4:
                    act.wait_ge(consts_done, N_CONST)
                    key_rms(0)
            softmax_exp(0)
            v_copy(0)
            rowsum(1, 0)
            rowsum(1, 1)
            p_copy(0)
            neg_mu(0)
            rowsum(1, 2)
            summed = NT + 3
            for t in range(B * NT):
                b, j = divmod(t, NT)
                if t and j == 0:
                    neg_mu(b)
                square(b, j)
                if j % G == G - 1:
                    first_rstd(b, j // G)
                for c in range(1, B):
                    if t == R_AT[c]:
                        r_copy(c)
                    if t == KK_AT[c]:
                        kk_sum(c)
                    if t == RMS_AT[c]:
                        key_rms(c)
                    if t == EXP_AT[c]:
                        softmax_exp(c)
                        v_copy(c)
                    if t == P_AT[c]:
                        p_copy(c)
                for _ in range(0 if t in NO_SUM else 2 if t in TWO_SUMS else 1):
                    if summed < B * NT:
                        rowsum(*divmod(summed, NT))
                        summed += 1

        @block.vector
        def _(dve):
            steps = [0]

            def const(ins):
                ins.then_inc(dconst, 1)
                steps[0] += 1
                dve.wait_ge(dconst, steps[0])

            dve.wait_ge(consts_done, N_CONST)
            const(dve.tensor_copy(identB[:, :], identF[:, :]))
            const(dve.memset(arow, 0.0))
            const(dve.memset(orow, 1.0))
            const(dve.memset(MC[:, :, :], 0.0))
            const(dve.memset(SM[:, :, :], 0.0))
            const(dve.memset(LT[:, :, :], 0.0))
            dve.memset(SM[:, :, ROW_ONE:ROW_ONE + 3], 1.0).then_inc(dconst, 1)
            steps[0] += 1
            dve.wait_ge(small_landed, 64)
            dve.tensor_tensor(x2[0:4, 1, 0:QK], x2[0:4, 1, 0:QK], x2[0:4, 1, QK:2 * QK], ALU.mult).then_inc(v_row, 1)
            dve.wait_ge(gb_psum, 1)
            const(dve.tensor_copy(GB[:, :, :], ps6[:, 0:2 * HC].rearrange("p (v c) -> p v c", v=2)))
            const(dve.tensor_copy(vv[:, :], ps6[:, QK:2 * QK]))
            const(dve.tensor_copy(gbp[:, 0, :, :], GB[:, :, :]))
            const(dve.tensor_tensor(pp[:, :, :], GB[:, :, :], gbp[:, 0, :, :], ALU.subtract))
            const(dve.tensor_copy(gbp[:, 1, :, :], pp[:, :, :]))
            const(dve.tensor_tensor(gbp[:, 2, :, :], pp[:, :, :], gbp[:, 1, :, :], ALU.subtract))

            def part_rows(v, at, reps):
                return (MC[:, :, at:at + 3 * reps].rearrange("p c (i j) -> p c i j", j=3),
                        gbp[:, :, v, :].rearrange("p j c -> p c j").unsqueeze(2).broadcast_to([P, HC, reps, 3]))

            o, i = part_rows(0, 0, 3)
            const(dve.tensor_copy(o, i))
            const(dve.memset(MC[:, :, ROW_ONE:ROW_ONE + 1], 1.0))
            dve.sem_inc(ma_ready, 1)

            def a_rows():
                dve.wait_ge(ra_psum, 1)
                const(dve.tensor_copy(RA, ps7[KR:2 * KR, :]))
                o, i = part_rows(0, ROW_M, 3)
                const(dve.tensor_copy(o, i))
                o, i = part_rows(1, ROW_ONE, 1)
                const(dve.tensor_copy(o, i))

            def rt_copy(b):
                dve.wait_ge(rt_psum, b + 1)
                src = psB[:, HALF:H].rearrange("p (c f u i) -> p c f u i", f=2, u=2, i=32)
                for f in range(2):
                    dst = rT[:, 4 * f:4 * f + 4, :].rearrange("p c (u i) -> p c u i", u=2)
                    dve.tensor_copy(dst, src[:, :, f, :, 0:16]).then_inc(rt_copied, 1)

            def score(b):
                dve.wait_ge(kk_summed, b + 1)
                dve.scalar_tensor_tensor(out=psB[:, 0:QK], in0=psB[:, 0:QK],
                                         scalar=1.0, in1=vv[:, :], op0=ALU.mult, op1=ALU.mult,
                                         accum_out=st[:, 0:1]).then_inc(kv_scored, 1)

            def row_ops(b):
                return lambda ins: ins.then_inc(row_step, 1), lambda n: dve.wait_ge(row_step, ROW_STEPS * b + n)

            def view8(ap):
                return ap.rearrange("o (u i) -> o u i", u=2)

            def row_a(b):
                done, after = row_ops(b)
                dve.wait_ge(rows_psum, b + 1)
                done(dve.tensor_copy(row, psum_rows))
                after(1)
                ss = row[:, 32:64].rearrange("o (u i) -> o u i", u=2)[:, :, 0:4]
                done(dve.tensor_scalar(view8(sc[0]), ss, 1.0 / H, EPS, ALU.mult, ALU.add))

            def row_b(b):
                done, after = row_ops(b)
                s = row[:, 0:32].rearrange("o (u i) -> o u i", u=2)[:, :, 0:4]
                dve.wait_ge(row_act, 4 * b + 2)
                done(dve.scalar_tensor_tensor(out=sc[3], in0=sc[0], scalar=-0.5, in1=sc[2],
                                              op0=ALU.mult, op1=ALU.mult))
                after(3)
                done(dve.tensor_tensor(sc[4], sc[3], sc[2], ALU.mult))
                after(4)
                done(dve.scalar_tensor_tensor(out=sc[1], in0=sc[4], scalar=1.5, in1=sc[2],
                                              op0=ALU.add, op1=ALU.mult))
                after(5)
                done(dve.tensor_tensor(view8(sc[3]), s, view8(sc[1]), ALU.mult))
                after(6)
                done(dve.reduce_max(sc[4][:, 0:1], sc[3], AX.X))
                after(7)
                done(dve.tensor_scalar(sc[5], sc[3], sc[4][:, 0:1], None, ALU.subtract))

            def row_c(b):
                done, after = row_ops(b)
                dve.wait_ge(row_act, 4 * b + 4)
                done(dve.reciprocal(sc[7][:, 1:2], sc[7][:, 0:1]))
                after(9)
                dst = arow.rearrange("o (q u i) -> o q u i", q=4, u=2)[:, :, :, 0:4]
                src = view8(sc[6]).unsqueeze(1).broadcast_to([1, 4, 2, 4])
                done(dve.tensor_scalar(dst, src, sc[7][:, 1:2], None, ALU.mult))

            def col_a(b):
                done, after = row_ops(b)
                dve.wait_ge(acol_psum, b + 1)
                done(dve.tensor_copy(attn[:, :], psum_attn))
                done(dve.tensor_tensor(acol[:, :], qmask[:, :], psum_attn[:, 0:4], ALU.mult))

            def col_b(b):
                done, after = row_ops(b)
                dve.wait_ge(pt_psum, b + 1)
                pt = psum_pt.rearrange("p (s q) -> p q s", s=2)
                kc = lambda ap: ap.rearrange("p (q s) -> p q s", s=2)
                done(dve.tensor_tensor(kc(pp[:, 1, :]), pt, kc(GB[:, 0, :]), ALU.mult))
                after(13)
                done(dve.tensor_copy(ppp[:, 0, :], pp[:, 1, :]))
                after(14)
                done(dve.tensor_tensor(pd[:, :], pp[:, 1, :], ppp[:, 0, :], ALU.subtract))
                after(15)
                done(dve.tensor_copy(ppp[:, 1, :], pd[:, :]))
                after(16)
                done(dve.tensor_tensor(ppp[:, 2, :], pd[:, :], ppp[:, 1, :], ALU.subtract))
                after(17)
                done(dve.tensor_copy(MC[:, :, 0:9].rearrange("p c (i j) -> p c i j", j=3),
                                     ppp[:, :, :].rearrange("p j c -> p c j").unsqueeze(2)
                                     .broadcast_to([P, HC, 3, 3])))

            def rc_copy(b, t=None):
                dve.wait_ge(rc_psum, b + 1)
                if t is not None:
                    dve.wait_ge(c_ready, t)
                c = C_AT[b % 2]
                dve.tensor_copy(ROWS[c:c + KR, H:2 * H], ps7[c:c + KR, :]).then_inc(rc_ready, 1)

            def lt_copy(b, g):
                dve.wait_ge(lt_psum, NG * b + g + 1)
                if b:
                    dve.wait_ge(c_ready, (b - 1) * NT + (g + 1) * G)
                dve.tensor_copy(LT[:, g, :], ps6h[0:K3, 0:G * P]).then_inc(lt_ready, 1)

            def mult(b, j):
                dve.wait_ge(a_ready, b * NT + j + 1)
                dve.tensor_tensor(x_tile(b, j), x_tile(b, j), psA[:, :], ALU.mult).then_inc(mult_done, 1)

            def add(b, j):
                dve.wait_ge(c_ready, b * NT + j + 1)
                dve.wait_ge(mult_done, b * NT + j + 1)
                dve.tensor_tensor(x_tile(b, j), x_tile(b, j), psC[:, :], ALU.add).then_inc(final_done, 1)

            def w_copy(m):
                WT = WkT if m < HC else WoT
                k = BLOCKS[m % HC]
                for h in range(2):
                    dve.wait_ge(w_psum, 2 * m + h + 1)
                    dve.tensor_copy(WT[:, 4 * h:4 * h + 4, k * P:(k + 1) * P],
                                    psC[:, h * HALF:(h + 1) * HALF].rearrange("p (c k) -> p c k", c=4)).then_inc(w_dve, 1)

            rt_copy(0)
            for m in range(1, 2 * HC, 2):
                w_copy(m)
                if m == 1:
                    a_rows()
                if m == HC + 3:
                    score(0)
                if m == HC + 5:
                    row_a(0)
            row_b(0)
            row_c(0)
            col_a(0)
            col_b(0)
            rt_copy(1)
            rc_copy(0)
            score(1)

            def chain_steps(place):
                for c in range(1, B):
                    k = place - START[c]
                    if k == VE["rt_copy"] and c > 1:
                        rt_copy(c)
                    if k == VE["score"] and c > 1:
                        score(c)
                    if k == VE["row_a"]:
                        row_a(c)
                    if k == VE["row_b"]:
                        row_b(c)
                    if k == VE["row_c"]:
                        row_c(c)
                    if k == VE["col_a"]:
                        col_a(c)
                    if k == VE["col_b"]:
                        col_b(c)
                    if k == VE["rc_copy"]:
                        rc_copy(c, place // 2)

            for place in range(START[1], 0):
                chain_steps(place)
            lt_copy(0, 0)
            for t in range(B * NT):
                b, j = divmod(t, NT)
                mult(b, j)
                if t % G == G - 1 and t + 1 < B * NT:
                    lt_copy(*divmod((t + 1) // G, NG))
                chain_steps(2 * t)
                if t:
                    add(*divmod(t - 1, NT))
                chain_steps(2 * t + 1)
            add(B - 1, NT - 1)

        @block.tensor
        def _(pe):
            mm = nc.tensor.matmul

            def sums(b, part):
                if part % 2 == 0:
                    pe.wait_ge(x_landed[b][part // 2], 16)
                for i in (part,):
                    for f in range(2):
                        for u in range(2):
                            q = 2 * f + u
                            at = (b * NT + 2 * i + u) * H + f * HALF
                            last = mm(psB[32 * q:32 * q + 32, 0:HALF], ones[:, 3 - i:35 - i],
                                      X[:, at:at + HALF], start=(i == 0), stop=(i == NT // 2 - 1))
                if part == NT // 2 - 1:
                    last.then_inc(r_summed, 1)

            def sums_t(b):
                pe.wait_ge(r_copied, b + 1)
                if b >= 2:
                    pe.wait_ge(p_ready, b)
                for c in range(4):
                    last = nc.tensor.transpose(psB[:, HALF + c * P:HALF + (c + 1) * P],
                                               RB[:, c * P:(c + 1) * P], identF[:, :])
                last.then_inc(rt_psum, 1)

            def times_w(at, WT, lo, n, chunks, done):
                for c in chunks:
                    for q in range(4):
                        k = q * QK + lo
                        last = mm(psB[32 * q:32 * q + 32, at + lo:at + lo + n], rT[:, c, :],
                                  WT[:, c, k:k + n], start=(c == 0), stop=(c == HC - 1))
                if done is not None and HC - 1 in chunks:
                    last.then_inc(done, 1)

            def keys(b, part):
                pe.wait_ge(rt_copied, 2 * (b + 1))
                times_w(0, WkT, 0, QK, range(2 * part, 2 * part + 2), k_done)

            def values(b, part):
                times_w(HALF, WoT, 0, QK, range(2 * part, 2 * part + 2), v_done)

            def rows(b):
                pe.wait_ge(kv_scored, b + 1)
                pe.wait_ge(kk_summed, b + 1)
                if b:
                    pe.wait_ge(rc_ready, b)
                mm(psum_rows[:, 0:32], st[:, 0:1], fold[:, :], start=True, stop=True)
                mm(psum_rows[:, 32:64], st[:, 1:2], fold[:, :], start=True, stop=True).then_inc(rows_psum, 1)

            def attn_col(b):
                pe.wait_ge(row_step, ROW_STEPS * b + 10)
                mm(psum_attn, arow, orow, start=True, stop=True).then_inc(acol_psum, 1)

            def p_rows(b):
                pe.wait_ge(row_step, ROW_STEPS * b + 12)
                pe.wait_ge(v_copied, b + 1)
                if b and b + 1 < B:
                    pe.wait_ge(r_copied, b + 2)
                at = (b % 2) * H + HALF
                for q in (0, 2, 1, 3):
                    if q == 1:
                        pe.wait_ge(p_halves, 2 * (b + 1))
                    mm((psB if b else psA)[:, q * QK:(q + 1) * QK], attn[32 * q:32 * q + 32, :],
                       Pb[32 * q:32 * q + 32, at:at + QK], start=True, stop=True).then_inc(
                        pb_psum if q % 2 else p_halves, 1)
                for s in range(2):
                    last = mm(psum_pt[:, 4 * s:4 * s + 4], Pb[:, at + s * P:at + (s + 1) * P], acol[:, :],
                              start=True, stop=True)
                last.then_inc(pt_psum, 1)

            def part_rows(lo, done):
                for c in range(HC):
                    last = nc.tensor.transpose(ps7[lo:lo + KR, c * P:(c + 1) * P], MC[:, c, :], identB[:, :])
                last.then_inc(done, 1)

            def c_rows(b):
                pe.wait_ge(row_step, ROW_STEPS * (b + 1))
                part_rows(C_AT[b % 2], rc_psum)

            def stat_rows(b, g):
                gi = NG * b + g
                pe.wait_ge(stat_step, STAT_STEPS * (gi + 1))
                for t in range(G):
                    for lo in (KR, C_AT[b % 2]):
                        last = nc.tensor.transpose(ps6h[lo:lo + KR, t * P:(t + 1) * P], SM[:, t, :], identB[:, :])
                lo = C_AT[1 - b % 2]
                last = mm(ps6[lo:lo + KR, 0:G * P // 2], ROWS[0:KR, 0:KR], ROWS[0:KR, 0:G * P // 2], start=True, stop=True)
                last.then_inc(lt_psum, 1)

            def outer(b, j, ps, at, ready, freed):
                t = b * NT + j
                pe.wait_ge(lt_ready, NG * b + j // G + 1)
                if t:
                    pe.wait_ge(freed, t)
                for f in range(2):
                    last = mm(ps[:, f * HALF:(f + 1) * HALF], LT[:, j // G, (j % G) * P:(j % G + 1) * P],
                              ROWS[0:K3, at + f * HALF:at + (f + 1) * HALF], start=True, stop=True)
                last.then_inc(ready, 1)

            def a_tile(b, j):
                outer(b, j, psA, 0, a_ready, mult_done)

            def c_tile(b, j):
                outer(b, j, psC, H, c_ready, final_done)

            def w_block(m):
                stage, landed = (2, wk_landed) if m < HC else (3, wo_landed)
                k = BLOCKS[m % HC]
                if m % 2 == 0:
                    pe.wait_ge(landed[m % HC // 2], 16)
                ps, freed = (psA, w_act) if m % 2 == 0 else (psC, w_dve)
                for h in range(2):
                    if m >= 2:
                        pe.wait_ge(freed, 2 * (m // 2 - 1) + h + 1)
                    for c in range(4 * h, 4 * h + 4):
                        at = (stage * NT + k) * H + c * P
                        last = nc.tensor.transpose(ps[:, c * P:(c + 1) * P], X[:, at:at + P], identF[:, :])
                    last.then_inc(w_psum, 1)

            def w_copied(m):
                pe.wait_ge(w_act, m)
                pe.wait_ge(w_dve, m)

            def warm(n):
                for _ in range(n):
                    mm(psC[:, 0:HALF], ROWS[0:K3, 0:P], ROWS[0:K3, 0:HALF], start=True, stop=True)

            pe.wait_ge(rows_zeroed, 1)
            warm(14)
            pe.wait_ge(ones_ready, 1)
            sums(0, 0)
            sums(0, 1)
            pe.wait_ge(consts_done, N_CONST)
            pe.wait_ge(small_landed, 64)
            nc.tensor.transpose(ps6[:, 0:2 * HC], x2[0:2 * HC, 0, 0:P], identF[0:2 * HC, 0:2 * HC])
            pe.wait_ge(v_row, 1)
            mm(ps6[:, QK:2 * QK], quad, x2[0:4, 1, 0:QK], start=True, stop=True).then_inc(gb_psum, 1)
            warm(8)
            sums(0, 2)
            sums(0, 3)
            sums_t(0)
            w_block(0)
            w_block(1)
            pe.wait_ge(ma_ready, 1)
            part_rows(KR, ra_psum)
            for m in range(2, 6):
                w_block(m)
            w_copied(4)
            pe.wait_ge(rt_copied, 2)
            times_w(0, WkT, 0, P, range(HC), None)
            for m in range(6, HC + 2):
                w_block(m)
            w_copied(HC)
            times_w(0, WkT, P, P, range(HC), k_done)
            for m in range(HC + 2, HC + 6):
                w_block(m)
            rows(0)
            w_copied(HC + 4)
            w_block(HC + 6)
            w_block(HC + 7)
            times_w(HALF, WoT, 0, P, range(HC), None)
            w_copied(2 * HC)
            times_w(HALF, WoT, P, P, range(HC), v_done)
            attn_col(0)
            p_rows(0)
            for part in range(4):
                sums(1, part)
            sums_t(1)
            c_rows(0)
            for part in range(4):
                keys(1, part)
            values(1, 0)
            values(1, 1)
            rows(1)
            values(1, 2)
            values(1, 3)
            stat_rows(0, 0)
            for part in range(3):
                sums(2, part)

            def chain_steps(place):
                for c in range(1, B):
                    k = place - START[c]
                    if c > 1:
                        if k == TE["sums_t"]:
                            sums_t(c)
                        if 0 <= k - TE["keys"] < 4:
                            keys(c, k - TE["keys"])
                        if k == TE["rows"]:
                            rows(c)
                        if 0 <= k - TE["values"] < 4:
                            values(c, k - TE["values"])
                    if k == TE["attn"]:
                        attn_col(c)
                    if c == 1 and place == 0:
                        sums(2, 3)
                    if c == 2 and 0 <= k - TE["sums"] < 4:
                        sums(3, k - TE["sums"])
                    if k == TE["p_rows"]:
                        p_rows(c)
                    if k == TE["c_rows"]:
                        c_rows(c)

            for place in range(START[1] + TE["attn"], 0):
                chain_steps(place)
            for t in range(B * NT):
                b, j = divmod(t, NT)
                a_tile(b, j)
                if t % G == G - 1 and t + 1 < B * NT:
                    stat_rows(*divmod((t + 1) // G, NG))
                chain_steps(2 * t)
                if t:
                    c_tile(*divmod(t - 1, NT))
                chain_steps(2 * t + 1)
            c_tile(B - 1, NT - 1)


_INS = ['x', 'cond_2048', 'L0_cond_rms_weight', 'L0_cond_Wk', 'L0_cond_Wo', 'L0_cond_ln_gamma', 'L0_cond_ln_beta']


def kernel(**inputs):
    import numpy as _np
    import concourse.bacc as _bacc
    from concourse.bass_utils import run_bass_kernel_spmd as _run

    nc = _bacc.Bacc("TRN2", target_bir_lowering=False, num_devices=1, dynamic_dma_scratch_size=256)
    arrays, args = {}, []
    for name in _INS:
        a = _np.ascontiguousarray(inputs[name])
        arrays[f"in_{name}_dram"] = a
        args.append(nc.dram_tensor(f"in_{name}_dram", a.shape, mybir.dt.from_np(a.dtype), kind="ExternalInput").ap())
    x = inputs['x']
    args.append(nc.dram_tensor("out_0_dram", x.shape, F32, kind="ExternalOutput").ap())
    bass_block_attention_residual_norm_kernel(nc, *args)
    r = _run(nc, [arrays], core_ids=[0])
    return r.results[0]["out_0_dram"]
```
